# Optimizing a Trainium2 kernel written in Bass

```python
import numpy as np
import jax
import jax.numpy as jnp

def _softmax(x, axis=-1):
    return jax.nn.softmax(x, axis=axis)

def _gelu(x):
    return jax.nn.gelu(x, approximate=True)

def _silu(x):
    return jax.nn.silu(x)

def _sigmoid(x):
    return jax.nn.sigmoid(x)

def _layernorm(x, axis=-1, eps=1e-05):
    m = jnp.mean(x, axis=axis, keepdims=True)
    v = jnp.var(x, axis=axis, keepdims=True)
    return (x - m) / jnp.sqrt(v + eps)

def _scatter_add(tgt, idx, src, axis=0):
    return tgt.at[idx].add(src)

def _segment_sum(src, seg, n):
    return jax.ops.segment_sum(src, seg, n)
kernel_name = 'mk_cond_seq_d2_seqx_r2_06de17'

def setup_inputs(seed: int=0):
    np.random.seed(seed)
    _w = jnp.asarray

    def _rec_inputs():
        import jax
        import jax.numpy as jnp
        _rk = jax.random.key(seed)
        x = 7.22e-05 + 1 * jax.random.normal(jax.random.fold_in(_rk, 1), (8, 512, 512), jnp.float32)
        _lenS = 512 - jax.random.randint(jax.random.fold_in(_rk, 7), (8,), 0, max(1, 512 // 4) + 1, jnp.int32)
        _lenS2 = 512 - jax.random.randint(jax.random.fold_in(_rk, 8), (8,), 0, max(1, 512 // 4) + 1, jnp.int32)
        cond_2048 = 0.00782532 + 1.00527 * jax.random.normal(jax.random.fold_in(_rk, 11), (8, 1024), jnp.float32)
        _validS = jnp.arange(512)[None, :] < _lenS[:, None]
        _validS2 = jnp.arange(512)[None, :] < _lenS2[:, None]
        _causal = jnp.tril(jnp.ones((512, 512), dtype=bool))
        mask_BxSx1_fk1 = jnp.where(jnp.ones((8, 512, 1), dtype=bool), 1.0, 0.0).astype(jnp.float32)
        return (x, cond_2048, mask_BxSx1_fk1)
    x, cond_2048, mask_BxSx1_fk1 = _rec_inputs()

    def _L0_cond_setup():
        import jax, jax.numpy as jnp
        import numpy as np
        B, T, D, H, TE = (4, 1024, 512, 8, 1024)
        EPS = 1e-05

        def _ln(x, w, b):
            m = jnp.mean(x, axis=-1, keepdims=True)
            v = jnp.mean((x - m) ** 2, axis=-1, keepdims=True)
            return (x - m) * jax.lax.rsqrt(v + EPS) * w + b
        key = jax.random.key(seed)
        ks = jax.random.split(key, 16)
        s = 0.02
        inp = {'x': jax.random.normal(ks[0], (B, T, D), jnp.float32), 'emb': jax.random.normal(ks[1], (B, TE), jnp.float32), 'src_mask': (jax.random.uniform(ks[2], (B, T, 1)) > 0.2).astype(jnp.float32), 'num_head': H, 'ln_w': jnp.ones((D,), jnp.float32), 'ln_b': jnp.zeros((D,), jnp.float32), 'Wq': jax.random.normal(ks[3], (D, D), jnp.float32) * s, 'bq': jnp.zeros((D,), jnp.float32), 'Wk': jax.random.normal(ks[4], (D, D), jnp.float32) * s, 'bk': jnp.zeros((D,), jnp.float32), 'Wv': jax.random.normal(ks[5], (D, D), jnp.float32) * s, 'bv': jnp.zeros((D,), jnp.float32), 'W_emb': jax.random.normal(ks[6], (TE, 2 * D), jnp.float32) * s, 'b_emb': jnp.zeros((2 * D,), jnp.float32), 'ln2_w': jnp.ones((D,), jnp.float32), 'ln2_b': jnp.zeros((D,), jnp.float32), 'W_out': jax.random.normal(ks[7], (D, D), jnp.float32) * s, 'b_out': jnp.zeros((D,), jnp.float32)}
        return inp
    _L0_cond_all = _L0_cond_setup()
    _L0_cond_in = {k: v for k, v in _L0_cond_all.items() if k in ('ln_w', 'ln_b', 'Wq', 'bq', 'Wk', 'bk', 'Wv', 'bv', 'W_emb', 'b_emb', 'ln2_w', 'ln2_b', 'W_out', 'b_out')}
    del _L0_cond_all

    def _L1_cond_setup():
        import jax, jax.numpy as jnp
        import numpy as np
        D = 512
        DI = 1024
        N = 16
        DT_RANK = 64
        D_CONV = 4
        EPS = 1e-05

        def _layernorm(x, g, b):
            mu = jnp.mean(x, axis=-1, keepdims=True)
            var = jnp.mean((x - mu) ** 2, axis=-1, keepdims=True)
            return (x - mu) * jax.lax.rsqrt(var + EPS) * g + b

        def _mamba(xn, in_proj_w, conv_w, conv_b, x_proj_w, dt_proj_w, dt_proj_b, A_log, D_param, out_proj_w):
            b, sl, _ = xn.shape
            xz = jnp.einsum('bsd,ed->bse', xn, in_proj_w)
            x_in, z = jnp.split(xz, 2, axis=-1)
            xt = jnp.transpose(x_in, (0, 2, 1))
            u = jax.lax.conv_general_dilated(xt, conv_w[:, None, :], (1,), [(D_CONV - 1, 0)], feature_group_count=DI, dimension_numbers=('NCH', 'OIH', 'NCH')) + conv_b[None, :, None]
            u = jax.nn.silu(jnp.transpose(u, (0, 2, 1)))
            x_dbl = jnp.einsum('bsd,ed->bse', u, x_proj_w)
            dt_r, B, C = jnp.split(x_dbl, [DT_RANK, DT_RANK + N], axis=-1)
            dt = jax.nn.softplus(jnp.einsum('bsr,dr->bsd', dt_r, dt_proj_w) + dt_proj_b)
            A = -jnp.exp(A_log)

            def step(h, inp):
                dt_t, B_t, C_t, u_t = inp
                dA = jnp.exp(dt_t[:, :, None] * A)
                h = h * dA + (dt_t * u_t)[:, :, None] * B_t[:, None, :]
                y = jnp.einsum('bdn,bn->bd', h, C_t)
                return (h, y)
            seq = (jnp.transpose(dt, (1, 0, 2)), jnp.transpose(B, (1, 0, 2)), jnp.transpose(C, (1, 0, 2)), jnp.transpose(u, (1, 0, 2)))
            h0 = jnp.zeros((b, DI, N), xn.dtype)
            _, ys = jax.lax.scan(step, h0, seq)
            y = jnp.transpose(ys, (1, 0, 2)) + u * D_param
            y = y * jax.nn.silu(z)
            return jnp.einsum('bsd,ed->bse', y, out_proj_w)
        key = jax.random.key(seed)
        ks = jax.random.split(key, 16)
        s = lambda fan: 1.0 / np.sqrt(fan)
        inp = {'x': jax.random.normal(ks[0], (2, 1024, D), jnp.float32), 'c': jax.random.normal(ks[1], (2, 2 * D), jnp.float32), 'ln_g': jnp.ones((D,), jnp.float32), 'ln_b': jnp.zeros((D,), jnp.float32), 'ada_w': jax.random.normal(ks[2], (3 * D, 2 * D), jnp.float32) * s(2 * D), 'ada_b': jnp.zeros((3 * D,), jnp.float32), 'in_proj_w': jax.random.normal(ks[3], (2 * DI, D), jnp.float32) * s(D), 'conv_w': jax.random.normal(ks[4], (DI, D_CONV), jnp.float32) * s(D_CONV), 'conv_b': jnp.zeros((DI,), jnp.float32), 'x_proj_w': jax.random.normal(ks[5], (DT_RANK + 2 * N, DI), jnp.float32) * s(DI), 'dt_proj_w': jax.random.normal(ks[6], (DI, DT_RANK), jnp.float32) * s(DT_RANK), 'dt_proj_b': jax.random.uniform(ks[7], (DI,), jnp.float32, -4.0, -2.0), 'A_log': jnp.tile(jnp.log(jnp.arange(1, N + 1, dtype=jnp.float32)), (DI, 1)), 'D_param': jnp.ones((DI,), jnp.float32), 'out_proj_w': jax.random.normal(ks[8], (D, DI), jnp.float32) * s(DI)}
        return inp
    _L1_cond_all = _L1_cond_setup()
    _L1_cond_in = {k: v for k, v in _L1_cond_all.items() if k in ('ln_g', 'ln_b', 'ada_w', 'ada_b', 'in_proj_w', 'conv_w', 'conv_b', 'x_proj_w', 'dt_proj_w', 'dt_proj_b', 'A_log', 'D_param', 'out_proj_w')}
    del _L1_cond_all
    return {'x': x, 'cond_2048': cond_2048, 'mask_BxSx1_fk1': mask_BxSx1_fk1, 'L0_cond_ln_w': _L0_cond_in['ln_w'], 'L0_cond_ln_b': _L0_cond_in['ln_b'], 'L0_cond_Wq': _L0_cond_in['Wq'], 'L0_cond_bq': _L0_cond_in['bq'], 'L0_cond_Wk': _L0_cond_in['Wk'], 'L0_cond_bk': _L0_cond_in['bk'], 'L0_cond_Wv': _L0_cond_in['Wv'], 'L0_cond_bv': _L0_cond_in['bv'], 'L0_cond_W_emb': _L0_cond_in['W_emb'], 'L0_cond_b_emb': _L0_cond_in['b_emb'], 'L0_cond_ln2_w': _L0_cond_in['ln2_w'], 'L0_cond_ln2_b': _L0_cond_in['ln2_b'], 'L0_cond_W_out': _L0_cond_in['W_out'], 'L0_cond_b_out': _L0_cond_in['b_out'], 'L1_cond_ln_g': _L1_cond_in['ln_g'], 'L1_cond_ln_b': _L1_cond_in['ln_b'], 'L1_cond_ada_w': _L1_cond_in['ada_w'], 'L1_cond_ada_b': _L1_cond_in['ada_b'], 'L1_cond_in_proj_w': _L1_cond_in['in_proj_w'], 'L1_cond_conv_w': _L1_cond_in['conv_w'], 'L1_cond_conv_b': _L1_cond_in['conv_b'], 'L1_cond_x_proj_w': _L1_cond_in['x_proj_w'], 'L1_cond_dt_proj_w': _L1_cond_in['dt_proj_w'], 'L1_cond_dt_proj_b': _L1_cond_in['dt_proj_b'], 'L1_cond_A_log': _L1_cond_in['A_log'], 'L1_cond_D_param': _L1_cond_in['D_param'], 'L1_cond_out_proj_w': _L1_cond_in['out_proj_w']}

def reference(x, cond_2048, mask_BxSx1_fk1, L0_cond_ln_w, L0_cond_ln_b, L0_cond_Wq, L0_cond_bq, L0_cond_Wk, L0_cond_bk, L0_cond_Wv, L0_cond_bv, L0_cond_W_emb, L0_cond_b_emb, L0_cond_ln2_w, L0_cond_ln2_b, L0_cond_W_out, L0_cond_b_out, L1_cond_ln_g, L1_cond_ln_b, L1_cond_ada_w, L1_cond_ada_b, L1_cond_in_proj_w, L1_cond_conv_w, L1_cond_conv_b, L1_cond_x_proj_w, L1_cond_dt_proj_w, L1_cond_dt_proj_b, L1_cond_A_log, L1_cond_D_param, L1_cond_out_proj_w):
    import jax
    import jax.numpy as jnp

    def _L0_cond_ref(x, emb, src_mask, num_head, ln_w, ln_b, Wq, bq, Wk, bk, Wv, bv, W_emb, b_emb, ln2_w, ln2_b, W_out, b_out):
        import jax, jax.numpy as jnp
        import numpy as np
        B, T, D, H, TE = (4, 1024, 512, 8, 1024)
        EPS = 1e-05

        def _ln(x, w, b):
            m = jnp.mean(x, axis=-1, keepdims=True)
            v = jnp.mean((x - m) ** 2, axis=-1, keepdims=True)
            return (x - m) * jax.lax.rsqrt(v + EPS) * w + b
        b, t, d = x.shape
        h = num_head
        dh = d // h
        xn = _ln(x, ln_w, ln_b)
        q = xn @ Wq + bq
        k = xn @ Wk + bk + (1.0 - src_mask) * -1000000.0
        q = jax.nn.softmax(q.reshape(b, t, h, dh), axis=-1)
        k = jax.nn.softmax(k.reshape(b, t, h, dh), axis=1)
        v = ((xn @ Wv + bv) * src_mask).reshape(b, t, h, dh)
        att = jnp.einsum('bnhd,bnhl->bhdl', k, v)
        y = jnp.einsum('bnhd,bhdl->bnhl', q, att).reshape(b, t, d)
        emb_out = (jax.nn.silu(emb) @ W_emb + b_emb)[:, None, :]
        scale, shift = jnp.split(emb_out, 2, axis=2)
        hh = _ln(y, ln2_w, ln2_b) * (1.0 + scale) + shift
        hh = jax.nn.silu(hh) @ W_out + b_out
        return x + hh

    def _L1_cond_ref(x, c, ln_g, ln_b, ada_w, ada_b, in_proj_w, conv_w, conv_b, x_proj_w, dt_proj_w, dt_proj_b, A_log, D_param, out_proj_w):
        import jax, jax.numpy as jnp
        import numpy as np
        D = 512
        DI = 1024
        N = 16
        DT_RANK = 64
        D_CONV = 4
        EPS = 1e-05

        def _layernorm(x, g, b):
            mu = jnp.mean(x, axis=-1, keepdims=True)
            var = jnp.mean((x - mu) ** 2, axis=-1, keepdims=True)
            return (x - mu) * jax.lax.rsqrt(var + EPS) * g + b

        def _mamba(xn, in_proj_w, conv_w, conv_b, x_proj_w, dt_proj_w, dt_proj_b, A_log, D_param, out_proj_w):
            b, sl, _ = xn.shape
            xz = jnp.einsum('bsd,ed->bse', xn, in_proj_w)
            x_in, z = jnp.split(xz, 2, axis=-1)
            xt = jnp.transpose(x_in, (0, 2, 1))
            u = jax.lax.conv_general_dilated(xt, conv_w[:, None, :], (1,), [(D_CONV - 1, 0)], feature_group_count=DI, dimension_numbers=('NCH', 'OIH', 'NCH')) + conv_b[None, :, None]
            u = jax.nn.silu(jnp.transpose(u, (0, 2, 1)))
            x_dbl = jnp.einsum('bsd,ed->bse', u, x_proj_w)
            dt_r, B, C = jnp.split(x_dbl, [DT_RANK, DT_RANK + N], axis=-1)
            dt = jax.nn.softplus(jnp.einsum('bsr,dr->bsd', dt_r, dt_proj_w) + dt_proj_b)
            A = -jnp.exp(A_log)

            def step(h, inp):
                dt_t, B_t, C_t, u_t = inp
                dA = jnp.exp(dt_t[:, :, None] * A)
                h = h * dA + (dt_t * u_t)[:, :, None] * B_t[:, None, :]
                y = jnp.einsum('bdn,bn->bd', h, C_t)
                return (h, y)
            seq = (jnp.transpose(dt, (1, 0, 2)), jnp.transpose(B, (1, 0, 2)), jnp.transpose(C, (1, 0, 2)), jnp.transpose(u, (1, 0, 2)))
            h0 = jnp.zeros((b, DI, N), xn.dtype)
            _, ys = jax.lax.scan(step, h0, seq)
            y = jnp.transpose(ys, (1, 0, 2)) + u * D_param
            y = y * jax.nn.silu(z)
            return jnp.einsum('bsd,ed->bse', y, out_proj_w)
        ada = jnp.einsum('bc,ec->be', jax.nn.silu(c), ada_w) + ada_b
        shift, scale, gate = jnp.split(ada, 3, axis=1)
        xn = _layernorm(x, ln_g, ln_b)
        xn = xn * (1.0 + scale[:, None, :]) + shift[:, None, :]
        x_ssm = _mamba(xn, in_proj_w, conv_w, conv_b, x_proj_w, dt_proj_w, dt_proj_b, A_log, D_param, out_proj_w)
        return x + gate[:, None, :] * x_ssm
    x = _L0_cond_ref(x, cond_2048, mask_BxSx1_fk1, 8, L0_cond_ln_w, L0_cond_ln_b, L0_cond_Wq, L0_cond_bq, L0_cond_Wk, L0_cond_bk, L0_cond_Wv, L0_cond_bv, L0_cond_W_emb, L0_cond_b_emb, L0_cond_ln2_w, L0_cond_ln2_b, L0_cond_W_out, L0_cond_b_out)
    x = _L1_cond_ref(x, cond_2048, L1_cond_ln_g, L1_cond_ln_b, L1_cond_ada_w, L1_cond_ada_b, L1_cond_in_proj_w, L1_cond_conv_w, L1_cond_conv_b, L1_cond_x_proj_w, L1_cond_dt_proj_w, L1_cond_dt_proj_b, L1_cond_A_log, L1_cond_D_param, L1_cond_out_proj_w)
    return x

_drawn_inputs = setup_inputs


def setup_inputs(seed=0):
    import zlib

    import numpy as np

    out = dict(_drawn_inputs(seed))
    spreads = {'L0_cond_ln_w': (1.0, 0.6),
     'L0_cond_ln_b': (0.0, 0.1),
     'L0_cond_bq': (0.0, 0.8),
     'L0_cond_bk': (0.0, 0.8),
     'L0_cond_bv': (0.0, 0.1),
     'L0_cond_b_emb': (0.0, 0.1),
     'L0_cond_ln2_w': (1.0, 0.2),
     'L0_cond_ln2_b': (0.0, 0.269),
     'L0_cond_b_out': (0.0, 0.1),
     'L1_cond_ln_g': (1.0, 0.2),
     'L1_cond_ln_b': (0.0, 0.1),
     'L1_cond_ada_b': (0.0, 0.1),
     'L1_cond_conv_b': (0.0, 0.1),
     'L1_cond_D_param': (1.0, 0.2)}
    factors = {'L0_cond_Wq': 8.0, 'L0_cond_Wk': 8.0}
    for name, (base, spread) in spreads.items():
        noise = np.random.default_rng([zlib.crc32(name.encode()), seed]).standard_normal(out[name].shape)
        drawn = base * np.exp(spread * noise) if base else spread * noise
        out[name] = jnp.asarray(drawn.astype(out[name].dtype))
    for name, factor in factors.items():
        out[name] = (out[name] * factor).astype(out[name].dtype)
    return out
```

```python
from contextlib import ExitStack

import concourse.bass as bass
from concourse import mybir

F32 = mybir.dt.float32
ALU = mybir.AluOpType
ACT = mybir.ActivationFunctionType
AX = mybir.AxisListType

P = 128
EPS = 1e-5
MASK_BIAS = 1e6


def build(nc, d):
    B, T, D = d["x"].shape
    TT, DT = T // P, D // P
    H = 8
    DH = D // H
    PAIRS = H // 2
    KC = d["cond"].shape[1]
    DI = d["w_out2"].shape[0]
    CT = DI // P
    N = 16
    R = 64
    XP = R + 2 * N
    NU = 2
    UN = N // NU
    NG = 4
    GN = N // NG
    WR = 4
    UB = CT * UN
    assert (TT, DT, CT, XP) == (4, 4, 8, 96)

    col, at = {}, 0
    for name, n in (("ln_w", DT), ("ln_b", DT), ("bk", DT), ("b_emb", 2 * DT), ("ln2_w", DT), ("ln2_b", DT),
                    ("g1", DT), ("b1", DT), ("b_ada", 3 * DT), ("conv_w", 4 * CT), ("conv_b", CT),
                    ("dt_b", CT), ("a_log", N * CT), ("d_par", CT), ("mask", B * TT)):
        col[name] = at
        at += n
    NCOL = at
    assert NCOL == d["cols"].shape[1]

    ctx = ExitStack()
    with ctx:
        def sb(name, n):
            return ctx.enter_context(nc.sbuf_tensor(name, [P, n], F32))

        def sem(name):
            return ctx.enter_context(nc.semaphore(name))

        cols = sb("cols", NCOL)
        ident = sb("ident", P)
        cond = sb("cond_sb", KC * B)
        embv = sb("embv", 2 * DT * B)
        adav = sb("adav", 2 * DT * B)
        scale0 = sb("scale0", B * DT)
        shift0 = sb("shift0", B * DT)
        scale1 = sb("scale1", B * DT)
        shift1 = sb("shift1", B * DT)
        cur = sb("cur", 5 * DT)
        neg_a = sb("neg_a", N * CT)
        stats = sb("stats", TT * 6)
        mv = sb("mv", TT * 2)
        rstd = sb("rstd", TT)
        nmr = sb("nmr", TT)
        minus_half = sb("minus_half", TT)
        spare = sb("spare", 1)
        eps_col = sb("eps_col", TT)
        zero_col = sb("zero_col", TT)
        var_eps = sb("var_eps", TT)
        stats3 = sb("stats3", TT * 6)
        mv3 = sb("mv3", TT * 2)
        rstd3 = sb("rstd3", TT)
        nmr3 = sb("nmr3", TT)
        stats2 = sb("stats2", TT * 6)
        mv2 = sb("mv2", TT * 2)
        rstd2 = sb("rstd2", TT)
        nmr2 = sb("nmr2", TT)

        w2 = sb("w2", DT * 2 * DI + CT * D + CT * XP + DI)
        w_ada = w2[:, 0:KC * 3 * D].rearrange("p (k n) -> p k n", k=KC)
        o = 0
        w_in = w2[:, o:o + DT * 2 * DI].rearrange("p (k n) -> p k n", k=DT)
        o += DT * 2 * DI
        w_out2 = w2[:, o:o + CT * D].rearrange("p (k n) -> p k n", k=CT)
        o += CT * D
        w_xp = w2[:, o:o + CT * XP].rearrange("p (k n) -> p k n", k=CT)
        o += CT * XP
        w_dt = w2[0:R, o:o + DI]

        TD = TT * D
        ARENA = 37888
        arena = sb("arena", ARENA)

        def views(*sizes):
            out, o = [], 0
            for n in sizes:
                out.append(arena[:, o:o + n])
                o += n
            assert o <= ARENA, o
            return out

        tiled = lambda a, k: a.rearrange("p (k n) -> p k n", k=k)
        (a_wk, a_wq, a_wv, a_wo, a_xr, a_sT, a_xh, a_xhT, a_xn, a_xnT, a_ekT, a_ek, a_q, a_eqT, a_v, a_y,
         a_att, bq_bc, bv_bc, bo_bc, maskrow, gate_sb, gate_b, a_sm) = views(
            *[DT * D] * 4, *[TD] * 12, PAIRS * P, D, D, D, T, D, D, 128)
        assert KC * 2 * D == 4 * TD
        a_wemb = arena[:, 4 * DT * D:4 * DT * D + 4 * TD]
        wk, wq, wv, wo = (tiled(a, DT) for a in (a_wk, a_wq, a_wv, a_wo))
        w_emb = tiled(a_wemb, KC)
        xn, xr, xh, ek, q_sb, v_sb, y_sb = (tiled(a, TT) for a in (a_xn, a_xr, a_xh, a_ek, a_q, a_v, a_y))
        xnT, ekT, eqT, sT, xhT = (tiled(a, DT) for a in (a_xnT, a_ekT, a_eqT, a_sT, a_xhT))
        att = tiled(a_att, PAIRS)
        nkmax, ksum, rksum = a_sm[:, 0:4], a_sm[:, 4:8], a_sm[:, 8:12]
        nqmax = a_sm[:, 16:48].rearrange("p (t h) -> p t h", t=TT)
        qsum = a_sm[:, 48:80].rearrange("p (t h) -> p t h", t=TT)
        rqsum = a_sm[:, 80:112].rearrange("p (t h) -> p t h", t=TT)

        (a_bb, a_cb, a_uy0, a_uy1, a_work, a_xmT0, a_xmT1, a_res, a_sz, a_dt, sp, gate_bc, xd, o_tmp) = views(
            N * T, N * T, CT * T, CT * T, WR * NU * T, TD, TD, 2 * D, 2 * T, 2 * T, T, D, T, D)
        b_bc, c_bc = tiled(a_bb, N), tiled(a_cb, N)
        uy = [tiled(a, CT) for a in (a_uy0, a_uy1)]
        work = a_work.rearrange("p (w n t) -> p w n t", w=WR, n=NU)
        xmT = [tiled(a, DT) for a in (a_xmT0, a_xmT1)]
        res, sz, dt = (tiled(a, 2) for a in (a_res, a_sz, a_dt))

        bankA = ctx.enter_context(nc.psum_tensor("bankA", [P, 4, 512], F32))
        bankB = ctx.enter_context(nc.psum_tensor("bankB", [P, 4, 512], F32))
        dA = bankA[:, :, :].rearrange("p (s n) t -> p s n t", s=2)
        dtu, ybank = bankB[:, 0, :], bankB[:, 1, :]
        gbank = [bankB[:, 2, :], bankB[:, 3, :]]

        S = {n: sem(n) for n in (
            "cols_in", "cond_in", "bc_in", "gate_b_in", "wk_in", "wq_in", "wv_in", "wo_in", "wemb_in", "wada_in", "w2_in",
            "ident_made", "sync_passed", "pre_step", "cond_act", "emb_mm", "ada_mm", "emb_col", "ada_col", "gate_row", "gate_stored", "nega",
            "x_in", "xr_in", "mask_in", "ln_step", "xn_done", "xnT_mm", "xnT_sb", "kT_mm", "kb_done", "kmax_done", "k_exp",
            "yT_mm", "sT_done", "cur0_set", "curm_set", "q_mm", "q_biased", "q_max", "q_shift", "q_exp", "q_sum", "q_rec", "wo_mm", "xr_biased",
            "x1_done", "x1_stored", "ln3_step", "ln_norm", "ln2_norm", "ln3_norm", "half_made", "xh_done", "xhT_mm", "xhT_sb", "xh_stored", "v_mm", "v_done", "mbv_done", "maskb_done", "ekt_mm", "ek_sb", "k_rec", "eqT_mm", "eqT_sb",
            "att_mm", "att_sb", "y_mm", "y_sb", "ln2_step", "yn_done",
            "dA_zeroed", "a_ready", "bx_done", "scanned", "hc_done", "reduced", "y_raw", "y_done", "dtu_done", "sp_step", "dt_done",
            "sz_done", "filled0", "filled1", "freed0", "freed1", "conv_a", "conv_tap", "u_done", "xm_in", "gbc_in",
            "xmT_done", "cur1_set", "xd_done", "bcd_stored", "o_scaled", "res_added")}
        res_in, out_stored = [sem("res_in0"), sem("res_in1")], [sem("out_stored0"), sem("out_stored1")]
        b_in, c_in = [sem(f"b_in{g}") for g in range(NG)], [sem(f"c_in{g}") for g in range(NG)]
        filled, freed = [S["filled0"], S["filled1"]], [S["freed0"], S["freed1"]]

        FILL = [["O0", "O1"], ["O2", "O3"], ["I0", "I1"], ["I2", "I3"], ["I4", "I5"],
                ["I6", "I7"], ["P"], []]

        def batch_jobs(first, last):
            out = []
            for c in range(CT):
                if not (last and c == CT - 1):
                    out.append(f"D{c + 1}")
                fill = [f for f in FILL[c] if not (first and f[0] == "O") and not (last and f[0] != "O")]
                out += fill
                if not (last and c == CT - 1):
                    out.append(f"Z{c + 1}")
            return out

        JOBS_A_BATCH = len(batch_jobs(False, False))
        number, n = {}, 0
        pre = [f"I{j}" for j in range(CT)] + ["P", "D0", "Z0"]
        for copy, jobs in (("pre", pre), ("first", batch_jobs(True, False)), ("odd", batch_jobs(False, False)),
                           ("even", batch_jobs(False, False))):
            for j in jobs:
                number[copy, j] = n
                n += 1
        n += (B // 2 - 2) * 2 * JOBS_A_BATCH
        for copy, jobs in (("last", batch_jobs(False, True)), ("post", ["O0", "O1", "O2", "O3"])):
            for j in jobs:
                number[copy, j] = n
                n += 1

        def job(copy, it, name, off=0):
            n = number[copy, name] + off
            k = n // 2
            return n % 2, (it * JOBS_A_BATCH + k if copy in ("odd", "even") else k)

        COPIES_LOOP = [("odd", 1), ("even", 2)]

        def l0_iterations(eng, body):
            body(0, False, True, True)
            body(1, True, True, True)
            with eng.Fori(2, B - 1) as i:
                body(i, True, True, True)
            body(B - 1, True, True, False)
            body(B, True, False, False)

        def l1_iterations(eng, body):
            body("first", 0, 0, 0, True, False)
            with eng.Fori(0, B // 2 - 1) as it:
                for copy, off in COPIES_LOOP:
                    body(copy, it, it * 2 + off, off % 2, False, False)
            body("last", 0, B - 1, (B - 1) % 2, False, True)

        def started(b):
            return not (isinstance(b, int) and b == 0)

        def second(b):
            return isinstance(b, int) and b == 1

        block = ctx.enter_context(nc.Block())

        @block.sync
        def _(sp_):
            sp_.dma_start(cols[:, :], d["cols"]).then_inc(S["cols_in"], 16)
            sp_.dma_start(xn, d["x"][0].rearrange("(t p) n -> p t n", p=P)).then_inc(S["x_in"], 16)
            for w, name, s in ((wk, "wk", "wk_in"), (wq, "wq", "wq_in"), (wv, "wv", "wv_in")):
                sp_.dma_start(w, d[name].rearrange("(k p) n -> p k n", p=P)).then_inc(S[s], 16)
            for t, name in ((bq_bc, "bq"), (bv_bc, "bv"), (bo_bc, "b_out")):
                sp_.dma_start(t, d[name].rearrange("(a n) -> a n", a=1).to_broadcast([P, D])).then_inc(S["bc_in"], 16)
            sp_.dma_start(cond[:, :], d["cond"].rearrange("p k b -> p (k b)")).then_inc(S["cond_in"], 16)
            sp_.dma_start(w_emb, d["w_emb"].rearrange("(k p) n -> p k n", p=P)).then_inc(S["wemb_in"], 16)
            sp_.dma_start(wo, d["wo"].rearrange("(k p) n -> p k n", p=P)).then_inc(S["wo_in"], 16)
            sp_.dma_start(gate_b[0:B, :], d["gate_b"].rearrange("(a n) -> a n", a=1).to_broadcast([B, D])).then_inc(S["gate_b_in"], 16)
            sp_.dma_start(w_ada, d["w_ada"].rearrange("(k p) n -> p k n", p=P)).then_inc(S["wada_in"], 16)

            def second_weights():
                sp_.wait_ge(S["gate_row"], 1)
                sp_.dma_start(d["gate_d"], gate_sb[0:B, :]).then_inc(S["gate_stored"], 16)
                sp_.dma_start(w_in, d["w_in"].rearrange("(k p) n -> p k n", p=P)).then_inc(S["w2_in"], 16)
                sp_.dma_start(w_out2, d["w_out2"].rearrange("(k p) n -> p k n", p=P)).then_inc(S["w2_in"], 16)
                sp_.dma_start(w_xp, d["w_xp"].rearrange("(k p) n -> p k n", p=P)).then_inc(S["w2_in"], 16)
                sp_.dma_start(w_dt, d["w_dt"]).then_inc(S["w2_in"], 16)

            def l0(i, prev, cur_, nxt):
                if cur_:
                    if started(i):
                        sp_.wait_ge(S["kb_done"], DT * i)
                        sp_.sem_inc(S["sync_passed"], 1)
                    sp_.dma_start(maskrow, d["mask"][bass.ds(i, 1), :].to_broadcast([P, T])).then_inc(S["mask_in"], 16)
                if prev:
                    if second(i):
                        sp_.wait_ge(S["emb_mm"], 1)
                    else:
                        sp_.wait_ge(S["x1_stored"], 16 * (i - 1))
                        sp_.sem_inc(S["sync_passed"], 1)
                        sp_.wait_ge(S["xh_done"], TT * (i - 1))
                        sp_.sem_inc(S["sync_passed"], 1)
                    sp_.dma_start(xr, d["x"][bass.ds(i - 1, 1), :, :].rearrange("a (t p) n -> p (a t) n", p=P)).then_inc(S["xr_in"], 16)
                if nxt:
                    sp_.wait_ge(S["xnT_mm"], DT * (i + 1))
                    sp_.sem_inc(S["sync_passed"], 1)
                    sp_.dma_start(xn, d["x"][bass.ds(i + 1, 1), :, :].rearrange("a (t p) n -> p (a t) n", p=P)).then_inc(S["x_in"], 16)
                if prev:
                    sp_.wait_ge(S["x1_done"], TT * i)
                    sp_.sem_inc(S["sync_passed"], 1)
                    sp_.dma_start(d["x1"][bass.ds(i - 1, 1), :, :].rearrange("a (t p) n -> p (a t) n", p=P), xr).then_inc(S["x1_stored"], 16)
                    sp_.wait_ge(S["xhT_sb"], DT * i)
                    sp_.sem_inc(S["sync_passed"], 1)
                    sp_.dma_start(d["xh"][bass.ds(i - 1, 1), :, :].rearrange("a (m p) t -> p (a m) t", p=P), xhT).then_inc(S["xh_stored"], 16)
                if not started(i):
                    second_weights()

            l0_iterations(sp_, l0)

            sp_.wait_ge(S["x1_stored"], 16 * B)

            sp_.wait_ge(S["xh_stored"], 16 * B)

            def load_xm(b, par):
                sp_.dma_start(xmT[par], d["xh"][bass.ds(b, 1), :, :].rearrange("a (m p) t -> p (a m) t", p=P)).then_inc(S["xm_in"], 16)

            def load_bc(b):
                sp_.wait_ge(S["xd_done"], b + 1)
                sp_.sem_inc(S["sync_passed"], 1)
                sp_.dma_start(d["bc_d"], xd[R:XP, :]).then_inc(S["bcd_stored"], 16)
                sp_.wait_ge(S["bcd_stored"], 16 * (b + 1))
                sp_.sem_inc(S["sync_passed"], 1)
                for g in range(NG):
                    rows = d["bc_d"].rearrange("n t -> (n t)").rearrange("(a m) -> a m", a=1)
                    if started(b):
                        sp_.wait_ge(S["bx_done"], UB * b - UN + 2 * (g + 1))
                        sp_.sem_inc(S["sync_passed"], 1)
                    sp_.dma_start(a_bb[:, g * GN * T:(g + 1) * GN * T], rows[:, g * GN * T:(g + 1) * GN * T].to_broadcast([P, GN * T])).then_inc(b_in[g], 16)
                    if started(b):
                        sp_.wait_ge(S["hc_done"], UB * b - UN + 2 * (g + 1))
                        sp_.sem_inc(S["sync_passed"], 1)
                    sp_.dma_start(a_cb[:, g * GN * T:(g + 1) * GN * T], rows[:, (N + g * GN) * T:(N + (g + 1) * GN) * T].to_broadcast([P, GN * T])).then_inc(c_in[g], 16)

            def outputs(b):
                rows = lambda name, t: d[name][bass.ds(b, 1), t * P:(t + 1) * P, :].rearrange("a p n -> p (a n)")
                if started(b):
                    sp_.wait_ge(S["o_scaled"], TT * b)
                    sp_.sem_inc(S["sync_passed"], 1)
                sp_.dma_start(gate_bc, d["gate_d"][bass.ds(b, 1), :].to_broadcast([P, D])).then_inc(S["gbc_in"], 16)
                for t in range(TT + 1):
                    if t < TT:
                        if t >= 2 or started(b):
                            sp_.wait_ge(out_stored[t % 2], 16 * (2 * b + t // 2))
                            sp_.sem_inc(S["sync_passed"], 1)
                        sp_.dma_start(res[:, t % 2, :], rows("x1", t)).then_inc(res_in[t % 2], 16)
                    if t >= 1:
                        sp_.wait_ge(S["res_added"], TT * b + t)
                        sp_.sem_inc(S["sync_passed"], 1)
                        sp_.dma_start(rows("out", t - 1), res[:, (t - 1) % 2, :]).then_inc(out_stored[(t - 1) % 2], 16)

            sp_.wait_ge(S["gate_stored"], 16)
            load_xm(0, 0)
            load_bc(0)

            def l1(copy, it, b, par, first, last):
                if not last:
                    if not first:
                        sp_.wait_ge(S["reduced"], UB * b)
                        sp_.sem_inc(S["sync_passed"], 1)
                    load_xm(b + 1, 1 - par)
                if not first:
                    outputs(b - 1)
                if not last:
                    load_bc(b + 1)

            l1_iterations(sp_, l1)
            outputs(B - 1)
            for o in out_stored:
                sp_.wait_ge(o, 16 * 2 * B)

        @block.tensor
        def _(pe):
            def transposes(out, blocks):
                for k, blk in enumerate(blocks):
                    mm = pe.transpose(out[:, k * P:(k + 1) * P], blk, ident[:, :])
                return mm

            def product(out, lhs, rhs, kt):
                for k in range(kt):
                    mm = pe.matmul(out, lhs(k), rhs(k), start=(k == 0), stop=(k == kt - 1))
                return mm

            def conditions():
                pe.wait_ge(S["cond_act"], 1)
                pe.wait_ge(S["wemb_in"], 16)
                pe.wait_ge(S["xnT_sb"], DT)
                cv = cond[:, :].rearrange("p (k b) -> p k b", k=KC)
                for m in range(2 * DT):
                    mm = product(bankA[:, 1, m * B:(m + 1) * B], lambda k: w_emb[:, k, m * P:(m + 1) * P], lambda k: cv[:, k, :], KC)
                mm.then_inc(S["emb_mm"], 1)
                pe.wait_ge(S["wada_in"], 16)
                for m in range(2 * DT):
                    product(bankA[:, 2, m * B:(m + 1) * B], lambda k: w_ada[:, k, m * P:(m + 1) * P], lambda k: cv[:, k, :], KC)
                product(bankA[0:B, 3, :], lambda k: cv[:, k, :], lambda k: w_ada[:, k, 2 * D:3 * D], KC).then_inc(S["ada_mm"], 1)

            def next_norm(i):
                pe.wait_ge(S["xh_done"], TT * i)
                for m in range(DT):
                    transposes(bankA[:, m, :], [xh[:, t, m * P:(m + 1) * P] for t in range(TT)]).then_inc(S["xhT_mm"], 1)

            def l0(i, prev, cur_, nxt):
                begun = started(i)
                if cur_:
                    pe.wait_ge(S["xn_done"], TT * (i + 1))
                    for m in range(DT):
                        if begun:
                            pe.wait_ge(S["ek_sb"], TT * i)
                            pe.wait_ge(S["att_sb"], 2 * i)
                            if not second(i):
                                pe.wait_ge(S["xhT_sb"], DT * (i - 1))
                        transposes(bankA[:, m, :], [xn[:, t, m * P:(m + 1) * P] for t in range(TT)]).then_inc(S["xnT_mm"], 1)
                    pe.wait_ge(S["xnT_sb"], DT * (i + 1))
                    if not begun:
                        pe.wait_ge(S["wk_in"], 16)
                    for m in range(DT):
                        if begun:
                            pe.wait_ge(S["y_sb"], TT * (i - 1) + m + 1)
                        product(bankB[:, m, :], lambda k: wk[:, k, m * P:(m + 1) * P], lambda k: xnT[:, k, :], DT).then_inc(S["kT_mm"], 1)
                if prev:
                    if not cur_:
                        pe.wait_ge(S["xhT_sb"], DT * (i - 1))
                    pe.wait_ge(S["yn_done"], TT * i)
                    for m in range(DT):
                        transposes(bankA[:, m, :], [y_sb[:, t, m * P:(m + 1) * P] for t in range(TT)]).then_inc(S["yT_mm"], 1)
                if cur_:
                    if not begun:
                        pe.wait_ge(S["wq_in"], 16)
                    for t in range(TT):
                        pe.wait_ge(S["kb_done"], DT * i + t + 1)
                        product(bankB[:, t, :], lambda k: xnT[:, k, t * P:(t + 1) * P], lambda k: wq[:, k, :], DT).then_inc(S["q_mm"], 1)
                if prev:
                    pe.wait_ge(S["sT_done"], DT * i)
                    for t in range(TT):
                        product(bankA[:, t, :], lambda k: sT[:, k, t * P:(t + 1) * P], lambda k: wo[:, k, :], DT).then_inc(S["wo_mm"], 1)
                if not cur_:
                    pe.wait_ge(S["x1_done"], TT * i)
                    next_norm(i)
                    return
                if not begun:
                    pe.wait_ge(S["wv_in"], 16)
                for t in range(TT):
                    pe.wait_ge(S["q_biased"], TT * i + t + 1)
                    product(bankB[:, t, :], lambda k: xnT[:, k, t * P:(t + 1) * P], lambda k: wv[:, k, :], DT).then_inc(S["v_mm"], 1)
                pe.wait_ge(S["k_exp"], DT * (i + 1))
                for t in range(TT):
                    if prev:
                        pe.wait_ge(S["x1_done"], TT * (i - 1) + t + 1)
                    transposes(bankA[:, t, :], [ekT[:, m, t * P:(t + 1) * P] for m in range(DT)]).then_inc(S["ekt_mm"], 1)
                pe.wait_ge(S["q_exp"], TT * (i + 1))
                for m in range(DT):
                    pe.wait_ge(S["v_done"], TT * i + m + 1)
                    transposes(bankB[:, m, :], [q_sb[:, t, m * P:(m + 1) * P] for t in range(TT)]).then_inc(S["eqT_mm"], 1)
                pe.wait_ge(S["ek_sb"], TT * (i + 1))
                for h in range(PAIRS):
                    mm = product(bankA[:, 0, h * P:(h + 1) * P], lambda t: ek[:, t, h * P:(h + 1) * P],
                                 lambda t: v_sb[:, t, h * P:(h + 1) * P], TT)
                mm.then_inc(S["att_mm"], 1)
                pe.wait_ge(S["att_sb"], 2 * (i + 1))
                pe.wait_ge(S["eqT_sb"], DT * (i + 1))
                for t in range(TT):
                    for h in range(PAIRS):
                        mm = pe.matmul(bankB[:, t, h * P:(h + 1) * P], eqT[:, h, t * P:(t + 1) * P], att[:, h, :], start=True, stop=True)
                    mm.then_inc(S["y_mm"], 1)
                if prev:
                    next_norm(i)
                if not begun:
                    conditions_after(pe)

            def conditions_after(pe):
                conditions()
                pe.wait_ge(S["emb_col"], 1)
                pe.wait_ge(S["ada_col"], 1)
                pe.wait_ge(S["gate_row"], 1)

            pe.wait_ge(S["ident_made"], 2)
            l0_iterations(pe, l0)

            pe.wait_ge(S["w2_in"], 64)
            pe.wait_ge(S["xhT_sb"], DT * B)
            pe.wait_ge(S["dA_zeroed"], 1)

            def run(copy, it, b, par, name):
                bank, before = job(copy, it, name)
                out = gbank[bank]
                if number[copy, name] >= 2:
                    pe.wait_ge(freed[bank], before)
                kind, j = name[0], int(name[1:] or 0)
                nb, npar = b + 1, 1 - par
                if copy == "pre":
                    nb, npar = 0, 0
                if kind == "I":
                    if j == 0:
                        pe.wait_ge(S["xmT_done"], DT * (nb + 1))
                    mm = product(out, lambda k: w_in[:, k, j * P:(j + 1) * P], lambda k: xmT[npar][:, k, :], DT)
                elif kind == "P":
                    pe.wait_ge(S["u_done"], CT * (nb + 1))
                    mm = product(out[0:XP, :], lambda k: w_xp[:, k, :], lambda k: uy[npar][:, k, :], CT)
                elif kind == "D":
                    if j in (0, CT):
                        pe.wait_ge(S["xd_done"], nb + 1)
                    c = j % CT
                    mm = pe.matmul(out, w_dt[:, c * P:(c + 1) * P], xd[0:R, :], start=True, stop=True)
                elif kind == "Z":
                    zp, c = (par, j) if j < CT and copy != "pre" else (npar, j % CT)
                    mm = product(out, lambda k: w_in[:, k, DI + c * P:DI + (c + 1) * P], lambda k: xmT[zp][:, k, :], DT)
                elif kind == "O":
                    ob, opar = (b - 1, 1 - par) if copy != "post" else (b, par)
                    if j == 0:
                        pe.wait_ge(S["y_done"], CT * (ob + 1))
                    mm = product(out, lambda k: uy[opar][:, k, j * P:(j + 1) * P], lambda k: w_out2[:, k, :], CT)
                mm.then_inc(filled[bank], 1)

            for name in pre:
                run("pre", 0, 0, 0, name)

            def l1(copy, it, b, par, first, last):
                jobs = batch_jobs(first, last)
                for c in range(CT):
                    step = [j for j in FILL[c] if j in jobs]
                    after = {k: [] for k in range(UN)}
                    for k, name in [(0, f"D{c + 1}"), *zip((2, 4) if c < 2 else (1, 3), step), (6, f"Z{c + 1}")]:
                        if name in jobs:
                            after[k].append(name)
                    for k in range(UN):
                        u = UB * b + c * UN + k
                        pe.wait_ge(S["hc_done"], u + 1)
                        if k == 0 and not (first and c == 0):
                            pe.wait_ge(S["y_raw"], CT * b + c)
                        for n in range(NU):
                            mm = pe.matmul(ybank, ident[:, :], work[:, (c * UN + k) % WR, n, :],
                                           start=(k == 0 and n == 0), stop=(k == UN - 1 and n == NU - 1))
                        mm.then_inc(S["reduced"], 1)
                        for name in after[k]:
                            run(copy, it, b, par, name)

            l1_iterations(pe, l1)
            for name in ("O0", "O1", "O2", "O3"):
                run("post", 0, B - 1, (B - 1) % 2, name)

        @block.scalar
        def _(act):
            act.wait_ge(S["cond_in"], 16)
            act.activation(cond[:, :], cond[:, :], ACT.Silu).then_inc(S["cond_act"], 1)
            act.wait_ge(S["cols_in"], 16)
            act.activation(neg_a[:, :], cols[:, col["a_log"]:col["a_log"] + N * CT], ACT.Exp).then_inc(S["nega"], 1)

            def normalise0(i):
                act.wait_ge(S["ln_norm"], 4 * (i + 1))
                for t in range(TT):
                    act.activation(xn[:, t, :], xn[:, t, :], ACT.Identity, scale=rstd[:, t:t + 1], bias=nmr[:, t:t + 1]).then_inc(S["xn_done"], 1)

            def l0(i, prev, cur_, nxt):
                if cur_:
                    for m in range(DT):
                        if started(i) and m == 0:
                            act.wait_ge(S["v_mm"], TT * i)
                        act.wait_ge(S["xnT_mm"], DT * i + m + 1)
                        act.activation(xnT[:, m, :], bankA[:, m, :], ACT.Identity, scale=cols[:, col["ln_w"] + m:col["ln_w"] + m + 1],
                                       bias=cols[:, col["ln_b"] + m:col["ln_b"] + m + 1]).then_inc(S["xnT_sb"], 1)
                    for m in range(DT):
                        act.wait_ge(S["kmax_done"], DT * i + m + 1)
                        act.activation(ekT[:, m, :], ekT[:, m, :], ACT.Exp, bias=nkmax[:, m:m + 1], accum_out=ksum[:, m:m + 1]).then_inc(S["k_exp"], 1)
                if prev:
                    act.wait_ge(S["cur0_set"], 2 * i)
                    for m in range(DT):
                        act.wait_ge(S["yT_mm"], DT * (i - 1) + m + 1)
                        if m == 0 and not second(i):
                            act.wait_ge(S["wo_mm"], TT * (i - 1))
                        act.activation(sT[:, m, :], bankA[:, m, :], ACT.Silu, scale=cur[:, m:m + 1], bias=cur[:, DT + m:DT + m + 1]).then_inc(S["sT_done"], 1)
                if cur_:
                    for t in range(TT):
                        act.wait_ge(S["q_shift"], TT * i + t + 1)
                        act.activation(q_sb[:, t, :], q_sb[:, t, :], ACT.Exp).then_inc(S["q_exp"], 1)
                    if nxt:
                        normalise0(i + 1)
                if prev:
                    act.wait_ge(S["ln3_norm"], 4 * i)
                    for t in range(TT):
                        if not second(i):
                            act.wait_ge(S["xhT_mm"], DT * (i - 1))
                        act.activation(xh[:, t, :], xr[:, t, :], ACT.Identity, scale=rstd3[:, t:t + 1], bias=nmr3[:, t:t + 1]).then_inc(S["xh_done"], 1)
                if cur_:
                    for m in range(DT):
                        act.wait_ge(S["eqT_mm"], DT * i + m + 1)
                        act.activation(eqT[:, m, :], bankB[:, m, :], ACT.Identity).then_inc(S["eqT_sb"], 1)
                    act.wait_ge(S["ln2_norm"], 4 * (i + 1))
                    for t in range(TT):
                        act.activation(y_sb[:, t, :], y_sb[:, t, :], ACT.Identity, scale=rstd2[:, t:t + 1], bias=nmr2[:, t:t + 1]).then_inc(S["yn_done"], 1)
                if prev:
                    for m in range(DT):
                        act.wait_ge(S["xhT_mm"], DT * (i - 1) + m + 1)
                        if m == 0 and not second(i):
                            act.wait_ge(S["xh_stored"], 16 * (i - 1))
                        act.activation(xhT[:, m, :], bankA[:, m, :], ACT.Identity).then_inc(S["xhT_sb"], 1)

            normalise0(0)
            l0_iterations(act, l0)

            def condition(b, par):
                act.wait_ge(S["cur1_set"], 2 * (b + 1))
                act.wait_ge(S["xm_in"], 16 * (b + 1))
                for m in range(DT):
                    act.activation(xmT[par][:, m, :], xmT[par][:, m, :], ACT.Identity, scale=cur[:, 3 * DT + m:3 * DT + m + 1],
                                   bias=cur[:, 4 * DT + m:4 * DT + m + 1]).then_inc(S["xmT_done"], 1)

            def conv_start(copy, it, name, b, npar):
                j = int(name[1])
                bank, before = job(copy, it, name)
                act.wait_ge(filled[bank], before + 1)
                act.activation(uy[npar][:, j, :], gbank[bank], ACT.Identity, scale=cols[:, col["conv_w"] + 4 * j + 3:col["conv_w"] + 4 * j + 4],
                               bias=cols[:, col["conv_b"] + j:col["conv_b"] + j + 1]).then_inc(S["conv_a"], 1)

            def conv_silu(b, npar, j):
                act.wait_ge(S["conv_tap"], 3 * (CT * b + j + 1))
                act.activation(uy[npar][:, j, :], uy[npar][:, j, :], ACT.Silu).then_inc(S["u_done"], 1)

            def evacuate_P(copy, it, b):
                bank, before = job(copy, it, "P")
                act.wait_ge(filled[bank], before + 1)
                if started(b):
                    act.wait_ge(S["bcd_stored"], 16 * b)
                act.activation(xd[0:XP, :], gbank[bank][0:XP, :], ACT.Identity).then_inc(S["xd_done"], 1)
                act.wait_ge(S["xd_done"], b + 1)
                act.sem_inc(freed[bank], 1)

            def softplus(copy, it, name, tile):
                bank, before = job(copy, it, name)
                c = int(name[1]) % CT
                bias = cols[:, col["dt_b"] + c:col["dt_b"] + c + 1]
                act.wait_ge(filled[bank], before + 1)
                if started(tile):
                    act.wait_ge(S["dt_done"], tile)
                    act.wait_ge(S["dtu_done"], tile)
                act.activation(dt[:, c % 2, :], gbank[bank], ACT.Relu, bias=bias)
                act.activation(sp, gbank[bank], ACT.Abs, bias=bias).then_inc(S["sp_step"], 1)
                act.wait_ge(S["sp_step"], 3 * tile + 1)
                act.sem_inc(freed[bank], 1)
                act.activation(sp, sp, ACT.Exp, scale=-1.0).then_inc(S["sp_step"], 1)
                act.wait_ge(S["sp_step"], 3 * tile + 2)
                act.activation(sp, sp, ACT.Ln, bias=1.0).then_inc(S["sp_step"], 1)

            def silu_z(copy, it, name, off, c, tile):
                bank, before = job(copy, it, name, off)
                act.wait_ge(filled[bank], before + 1)
                if not (isinstance(tile, int) and tile < 2):
                    act.wait_ge(S["y_done"], tile - 1)
                act.activation(sz[:, c % 2, :], gbank[bank], ACT.Silu).then_inc(S["sz_done"], 1)
                act.wait_ge(S["sz_done"], tile + 1)
                act.sem_inc(freed[bank], 1)

            act.wait_ge(S["xh_stored"], 16 * B)
            act.wait_ge(S["dA_zeroed"], 1)
            condition(0, 0)
            for j in range(CT):
                conv_start("pre", 0, f"I{j}", 0, 0)
                if j:
                    conv_silu(0, 0, j - 1)
            conv_silu(0, 0, CT - 1)
            evacuate_P("pre", 0, 0)
            softplus("pre", 0, "D0", 0)

            def l1(copy, it, b, par, first, last):
                for c in range(CT):
                    tile = CT * b + c
                    for k in range(UN):
                        u = UB * b + c * UN + k
                        if k == 0:
                            act.wait_ge(S["dt_done"], tile + 1)
                        if not (first and c == 0 and k < 2):
                            act.wait_ge(S["scanned"], u - 1)
                        for n in range(NU):
                            s = neg_a[:, c * N + NU * k + n:c * N + NU * k + n + 1]
                            e = act.activation(dA[:, k % 2, n, 1:T], dt[:, c % 2, 1:T], ACT.Exp, scale=s)
                        e.then_inc(S["a_ready"], 1)
                        if k == 1:
                            if c == 0:
                                zc = (copy, it, "D1", -1)
                            else:
                                zc = (copy, it, f"Z{c}", 0)
                            silu_z(*zc, c, tile)
                            if not last and 3 <= c <= 6:
                                conv_silu(b + 1, 1 - par, 2 * (c - 3))
                                conv_silu(b + 1, 1 - par, 2 * (c - 3) + 1)
                        if k == 3 and not (last and c == CT - 1):
                            softplus(copy, it, f"D{c + 1}", tile + 1)
                        if k == 4 and not last and 2 <= c <= 5:
                            conv_start(copy, it, f"I{2 * (c - 2)}", b + 1, 1 - par)
                        if k == 6 and not last and 2 <= c <= 5:
                            conv_start(copy, it, f"I{2 * (c - 2) + 1}", b + 1, 1 - par)
                        if k == 5 and not last and c == 0:
                            condition(b + 1, 1 - par)
                        if k == 4 and not last and c == 6:
                            evacuate_P(copy, it, b + 1)

            l1_iterations(act, l1)

        @block.vector
        def _(dve):
            def column(name, j):
                return cols[:, col[name] + j:col[name] + j + 1]

            def moments(src, st, m_v, s, before):
                for t in range(TT):
                    e = dve.bn_stats(st[:, 6 * t:6 * t + 6], src[:, t, :])
                e.then_inc(s, 1)
                dve.wait_ge(s, before + 1)
                dve.memset(spare[:, :], 0.0)
                for t in range(TT):
                    e = dve.bn_aggr(m_v[:, 2 * t:2 * t + 2], st[:, 6 * t:6 * t + 6])
                e.then_inc(s, 1)

            dve.memset(a_att, 0.0).then_inc(S["pre_step"], 1)
            dve.wait_ge(S["x_in"], 16)
            moments(xn, stats, mv, S["ln_step"], 0)
            dve.wait_ge(S["nega"], 1)
            dve.tensor_scalar(neg_a[:, :], neg_a[:, :], -1.0, None, ALU.mult).then_inc(S["nega"], 1)

            def columns():
                v = embv[:, :].rearrange("p (m b) -> p m b", m=2 * DT)
                a = adav[:, :].rearrange("p (m b) -> p m b", m=2 * DT)

                def vec(name, n=DT):
                    return cols[:, col[name]:col[name] + n].rearrange("p (m a) -> p m a", a=1).to_broadcast([P, n, B])

                dve.wait_ge(S["emb_mm"], 1)
                dve.tensor_tensor(v, bankA[:, 1, 0:2 * DT * B].rearrange("p (m b) -> p m b", b=B), vec("b_emb", 2 * DT), ALU.add).then_inc(S["emb_col"], 1)
                dve.wait_ge(S["ada_mm"], 1)
                dve.tensor_tensor(a, bankA[:, 2, 0:2 * DT * B].rearrange("p (m b) -> p m b", b=B), vec("b_ada", 2 * DT), ALU.add).then_inc(S["ada_col"], 1)
                dve.wait_ge(S["gate_b_in"], 16)
                dve.tensor_tensor(gate_sb[0:B, :], bankA[0:B, 3, :], gate_b[0:B, :], ALU.add).then_inc(S["gate_row"], 1)
                dve.wait_ge(S["emb_col"], 1)
                dve.wait_ge(S["ada_col"], 1)
                by_batch = lambda x: x[:, :].rearrange("p (b m) -> p m b", b=B)
                for n, (out_scale, out_shift, scale, shift, w, b) in enumerate((
                        (scale0, shift0, v[:, 0:DT, :], v[:, DT:, :], "ln2_w", "ln2_b"),
                        (scale1, shift1, a[:, DT:, :], a[:, 0:DT, :], "g1", "b1"))):
                    dve.tensor_scalar(scale, scale, 1.0, None, ALU.add).then_inc(S["pre_step"], 1)
                    dve.wait_ge(S["pre_step"], 4 * n + 2)
                    dve.tensor_tensor(by_batch(out_scale), scale, vec(w), ALU.mult).then_inc(S["pre_step"], 1)
                    dve.tensor_tensor(by_batch(out_shift), scale, vec(b), ALU.mult).then_inc(S["pre_step"], 1)
                    dve.wait_ge(S["pre_step"], 4 * n + 4)
                    dve.tensor_tensor(by_batch(out_shift), by_batch(out_shift), shift, ALU.add).then_inc(S["pre_step"], 1)
                dve.wait_ge(S["pre_step"], 9)

            def heads(x):
                return x.rearrange("p (h e) -> p h e", h=H)

            def spread(x, n):
                return x.rearrange("p (h a) -> p h a", a=1).to_broadcast([P, H, n])

            def l0(i, prev, cur_, nxt):
                begun = started(i)
                if prev:
                    if not second(i):
                        dve.wait_ge(S["sT_done"], DT * (i - 1))
                    dve.tensor_copy(cur[:, 0:DT], scale0[:, bass.ds((i - 1) * DT, DT)]).then_inc(S["cur0_set"], 1)
                    dve.tensor_copy(cur[:, DT:2 * DT], shift0[:, bass.ds((i - 1) * DT, DT)]).then_inc(S["cur0_set"], 1)
                if cur_:
                    if begun:
                        dve.wait_ge(S["mbv_done"], i)
                    else:
                        dve.wait_ge(S["cols_in"], 16)
                    dve.tensor_copy(cur[:, 2 * DT:3 * DT], cols[:, bass.ds(i * TT + col["mask"], TT)]).then_inc(S["curm_set"], 1)
                    dve.wait_ge(S["mask_in"], 16 * (i + 1))
                    dve.tensor_scalar(maskrow, maskrow, 1.0, MASK_BIAS, ALU.subtract, ALU.mult).then_inc(S["maskb_done"], 1)
                    for m in range(DT):
                        dve.wait_ge(S["kT_mm"], DT * i + m + 1)
                        if m == 0:
                            dve.wait_ge(S["maskb_done"], i + 1)
                            if begun:
                                dve.wait_ge(S["ekt_mm"], TT * i)
                        dve.scalar_tensor_tensor(ekT[:, m, :], bankB[:, m, :], column("bk", m), maskrow, ALU.add, ALU.add).then_inc(S["kb_done"], 1)
                        dve.wait_ge(S["kb_done"], DT * i + m + 1)
                        dve.tensor_reduce(nkmax[:, m:m + 1], ekT[:, m, :], AX.X, ALU.max, negate=True).then_inc(S["kmax_done"], 1)
                    for t in range(TT):
                        dve.wait_ge(S["q_mm"], TT * i + t + 1)
                        if t == 0:
                            dve.wait_ge(S["bc_in"], 48)
                            if begun:
                                dve.wait_ge(S["eqT_mm"], DT * i)
                        dve.tensor_tensor(q_sb[:, t, :], bankB[:, t, :], bq_bc, ALU.add).then_inc(S["q_biased"], 1)
                        dve.wait_ge(S["q_biased"], TT * i + t + 1)
                        dve.tensor_reduce(nqmax[:, t, :], heads(q_sb[:, t, :]), AX.X, ALU.max, negate=True).then_inc(S["q_max"], 1)
                if prev:
                    dve.wait_ge(S["xr_biased"], i)
                    for t in range(TT):
                        dve.wait_ge(S["wo_mm"], TT * (i - 1) + t + 1)
                        dve.tensor_tensor(xr[:, t, :], bankA[:, t, :], xr[:, t, :], ALU.add).then_inc(S["x1_done"], 1)
                    dve.wait_ge(S["x1_done"], TT * i)
                    moments(xr, stats3, mv3, S["ln3_step"], 2 * (i - 1))
                if not cur_:
                    return
                dve.wait_ge(S["curm_set"], i + 1)
                for t in range(TT):
                    dve.wait_ge(S["v_mm"], TT * i + t + 1)
                    if t == 0:
                        dve.wait_ge(S["mbv_done"], i + 1)
                    dve.scalar_tensor_tensor(v_sb[:, t, :], bankB[:, t, :], cur[:, 2 * DT + t:2 * DT + t + 1], v_sb[:, t, :],
                                             ALU.mult, ALU.add).then_inc(S["v_done"], 1)
                if nxt:
                    dve.wait_ge(S["x_in"], 16 * (i + 2))
                    moments(xn, stats, mv, S["ln_step"], 2 * (i + 1))
                dve.wait_ge(S["k_exp"], DT * (i + 1))
                dve.reciprocal(rksum, ksum).then_inc(S["k_rec"], 1)
                for t in range(TT):
                    dve.wait_ge(S["ekt_mm"], TT * i + t + 1)
                    dve.tensor_copy(ek[:, t, :], bankA[:, t, :]).then_inc(S["ek_sb"], 1)
                for t in range(TT):
                    dve.wait_ge(S["q_exp"], TT * i + t + 1)
                    dve.tensor_reduce(qsum[:, t, :], heads(q_sb[:, t, :]), AX.X, ALU.add).then_inc(S["q_sum"], 1)
                dve.wait_ge(S["q_sum"], TT * (i + 1))
                dve.reciprocal(a_sm[:, 80:112], a_sm[:, 48:80]).then_inc(S["q_rec"], 1)
                dve.wait_ge(S["att_mm"], i + 1)
                dve.wait_ge(S["k_rec"], i + 1)
                pa = bankA[:, 0, :].rearrange("p (h e) -> p h e", h=PAIRS)
                for s in range(2):
                    rows = slice(s * DH, (s + 1) * DH)
                    rk = rksum[rows, :].rearrange("p (h a) -> p h a", a=1).to_broadcast([DH, PAIRS, DH])
                    dve.tensor_tensor(att[rows, :, s * DH:(s + 1) * DH], pa[rows, :, s * DH:(s + 1) * DH], rk, ALU.mult).then_inc(S["att_sb"], 1)
                dve.wait_ge(S["q_rec"], i + 1)
                for t in range(TT):
                    dve.wait_ge(S["y_mm"], TT * i + t + 1)
                    dve.tensor_tensor(heads(y_sb[:, t, :]), heads(bankB[:, t, :]), spread(rqsum[:, t, :], DH), ALU.mult).then_inc(S["y_sb"], 1)
                dve.wait_ge(S["y_sb"], TT * (i + 1))
                moments(y_sb, stats2, mv2, S["ln2_step"], 2 * i)
                if not begun:
                    columns()

            l0_iterations(dve, l0)

            dve.wait_ge(S["xh_stored"], 16 * B)
            dve.memset(dA[:, :, :, 0:1], 0.0).then_inc(S["dA_zeroed"], 1)

            def condition_columns(b):
                if started(b):
                    dve.wait_ge(S["xmT_done"], DT * b)
                dve.tensor_copy(cur[:, 3 * DT:4 * DT], scale1[:, bass.ds(b * DT, DT)]).then_inc(S["cur1_set"], 1)
                dve.tensor_copy(cur[:, 4 * DT:5 * DT], shift1[:, bass.ds(b * DT, DT)]).then_inc(S["cur1_set"], 1)

            def taps(copy, it, name, b, npar):
                j = int(name[1])
                bank, before = job(copy, it, name)
                dve.wait_ge(S["conv_a"], CT * b + j + 1)
                u = uy[npar][:, j, :]
                for s in range(1, 4):
                    dve.scalar_tensor_tensor(u[:, s:T], gbank[bank][:, 0:T - s], column("conv_w", 4 * j + 3 - s), u[:, s:T],
                                             ALU.mult, ALU.add).then_inc(S["conv_tap"], 1)
                    dve.wait_ge(S["conv_tap"], 3 * (CT * b + j) + s)
                dve.sem_inc(freed[bank], 1)

            def make_dtu(b, par, c):
                tile = CT * b + c
                dve.wait_ge(S["dt_done"], tile + 1)
                if c == 0:
                    dve.wait_ge(S["u_done"], CT * (b + 1))
                if c or started(b):
                    dve.wait_ge(S["bx_done"], tile * UN)
                dve.tensor_tensor(dtu, dt[:, c % 2, :], uy[par][:, c, :], ALU.mult).then_inc(S["dtu_done"], 1)
                dve.wait_ge(S["dtu_done"], tile + 1)

            def times_b(b, c, k, started_):
                u = UB * b + c * UN + k
                if started_:
                    dve.wait_ge(S["reduced"], u - WR + 1)
                if c == 0 and k % 2 == 0:
                    dve.wait_ge(b_in[k // 2], 16 * (b + 1))
                two = dtu.rearrange("p (a t) -> p a t", a=1).to_broadcast([P, NU, T])
                dve.tensor_tensor(work[:, (c * UN + k) % WR, :, :], two, b_bc[:, NU * k:NU * (k + 1), :], ALU.mult).then_inc(S["bx_done"], 1)

            def gate_y(b, par, c):
                dve.wait_ge(S["reduced"], UB * b + (c + 1) * UN)
                dve.scalar_tensor_tensor(uy[par][:, c, :], uy[par][:, c, :], column("d_par", c), ybank, ALU.mult, ALU.add).then_inc(S["y_raw"], 1)

            def output(copy, it, name, b):
                t = int(name[1])
                bank, before = job(copy, it, name)
                dve.wait_ge(filled[bank], before + 1)
                if t == 0:
                    dve.wait_ge(S["gbc_in"], 16 * (b + 1))
                n = TT * b + t
                if t or started(b):
                    dve.wait_ge(S["res_added"], n)
                dve.tensor_tensor(o_tmp, gbank[bank], gate_bc, ALU.mult).then_inc(S["o_scaled"], 1)
                dve.wait_ge(S["o_scaled"], n + 1)
                dve.sem_inc(freed[bank], 1)

            condition_columns(0)
            for j in range(CT):
                taps("pre", 0, f"I{j}", 0, 0)
            make_dtu(0, 0, 0)
            times_b(0, 0, 0, False)

            def l1(copy, it, b, par, first, last):
                for c in range(CT):
                    for k in range(UN):
                        if k < UN - 1:
                            times_b(b, c, k + 1, not (first and c == 0 and k + 1 < WR))
                        elif c < CT - 1:
                            make_dtu(b, par, c + 1)
                            times_b(b, c + 1, 0, True)
                        elif not last:
                            make_dtu(b + 1, 1 - par, 0)
                            times_b(b + 1, 0, 0, True)
                        u = UB * b + c * UN + k
                        w = work[:, (c * UN + k) % WR, :, :].rearrange("p n t -> p (n t)")
                        dve.wait_ge(S["bx_done"], u + 1)
                        dve.wait_ge(S["a_ready"], u + 1)
                        dve.tensor_tensor_scan(w, dA[:, k % 2, :, :].rearrange("p n t -> p (n t)"), w, 0.0, ALU.mult, ALU.add).then_inc(S["scanned"], 1)
                        if k == 0:
                            if c > 0:
                                gate_y(b, par, c - 1)
                            elif not first:
                                gate_y(b - 1, 1 - par, CT - 1)
                        if not last:
                            if c == 0 and k == 2:
                                condition_columns(b + 1)
                            if 2 <= c <= 5 and k == 4:
                                taps(copy, it, f"I{2 * (c - 2)}", b + 1, 1 - par)
                            if 2 <= c <= 5 and k == 6:
                                taps(copy, it, f"I{2 * (c - 2) + 1}", b + 1, 1 - par)
                        if not first and c < 2 and k in (4, 6):
                            output(copy, it, f"O{2 * c + (k == 6)}", b - 1)

            l1_iterations(dve, l1)
            gate_y(B - 1, (B - 1) % 2, CT - 1)
            for t in range(TT):
                output("post", 0, f"O{t}", B - 1)

        @block.gpsimd
        def _(pool):
            pool.memset(ident[:, :], 0.0).then_inc(S["ident_made"], 1)
            pool.wait_ge(S["ident_made"], 1)
            pool.affine_select(out=ident[:, :], in_=ident[:, :], compare_op=ALU.not_equal, fill=1.0, base=0,
                               pattern=[[-1, P]], channel_multiplier=1).then_inc(S["ident_made"], 1)
            pool.memset(minus_half[:, :], -0.5).then_inc(S["half_made"], 1)
            pool.memset(eps_col[:, :], EPS).then_inc(S["half_made"], 1)
            pool.memset(zero_col[:, :], 0.0).then_inc(S["half_made"], 1)
            pool.wait_ge(S["half_made"], 3)

            def norm_factors(m_v, rs, nm, made, s, n):
                pairs = m_v[:, :].rearrange("p (t two) -> p t two", two=2)
                pool.wait_ge(made, 2 * (n + 1))
                pool.tensor_tensor(var_eps[:, :], pairs[:, :, 1], eps_col[:, :], ALU.add).then_inc(s, 1)
                pool.wait_ge(s, 4 * n + 1)
                pool.tensor_tensor(rs[:, :], var_eps[:, :], minus_half[:, :], ALU.pow).then_inc(s, 1)
                pool.wait_ge(s, 4 * n + 2)
                pool.tensor_tensor(nm[:, :], pairs[:, :, 0], rs[:, :], ALU.mult).then_inc(s, 1)
                pool.wait_ge(s, 4 * n + 3)
                pool.tensor_tensor(nm[:, :], zero_col[:, :], nm[:, :], ALU.subtract).then_inc(s, 1)

            norm_factors(mv, rstd, nmr, S["ln_step"], S["ln_norm"], 0)
            pool.wait_ge(S["bc_in"], 48)

            def l0(i, prev, cur_, nxt):
                if cur_:
                    pool.wait_ge(S["curm_set"], i + 1)
                    if started(i):
                        pool.wait_ge(S["att_mm"], i)
                    for t in range(TT):
                        e = pool.tensor_tensor(v_sb[:, t, :], bv_bc, cur[:, 2 * DT + t:2 * DT + t + 1].to_broadcast([P, D]), ALU.mult)
                    e.then_inc(S["mbv_done"], 1)
                if prev:
                    pool.wait_ge(S["xr_in"], 16 * i)
                    pool.tensor_tensor(xr, xr, bo_bc.rearrange("p (a n) -> p a n", a=1).to_broadcast([P, TT, D]), ALU.add).then_inc(S["xr_biased"], 1)
                if cur_:
                    for t in range(TT):
                        pool.wait_ge(S["q_max"], TT * i + t + 1)
                        q = q_sb[:, t, :].rearrange("p (h e) -> p h e", h=H)
                        m = nqmax[:, t, :].rearrange("p (h a) -> p h a", a=1).to_broadcast([P, H, DH])
                        pool.tensor_tensor(q, q, m, ALU.add).then_inc(S["q_shift"], 1)
                if prev:
                    norm_factors(mv3, rstd3, nmr3, S["ln3_step"], S["ln3_norm"], i - 1)
                if nxt:
                    norm_factors(mv, rstd, nmr, S["ln_step"], S["ln_norm"], i + 1)
                if cur_:
                    norm_factors(mv2, rstd2, nmr2, S["ln2_step"], S["ln2_norm"], i)

            l0_iterations(pool, l0)

            def add_dt(tile, c):
                pool.wait_ge(S["sp_step"], 3 * (tile + 1))
                pool.tensor_tensor(dt[:, c % 2, :], dt[:, c % 2, :], sp, ALU.add).then_inc(S["dt_done"], 1)

            def gate(b, par, c):
                tile = CT * b + c
                pool.wait_ge(S["y_raw"], tile + 1)
                pool.wait_ge(S["sz_done"], tile + 1)
                pool.tensor_tensor(uy[par][:, c, :], uy[par][:, c, :], sz[:, c % 2, :], ALU.mult).then_inc(S["y_done"], 1)

            def residual(b, t):
                pool.wait_ge(S["o_scaled"], TT * b + t + 1)
                pool.wait_ge(res_in[t % 2], 16 * (2 * b + t // 2 + 1))
                pool.tensor_tensor(res[:, t % 2, :], res[:, t % 2, :], o_tmp, ALU.add).then_inc(S["res_added"], 1)

            add_dt(0, 0)

            def l1(copy, it, b, par, first, last):
                for c in range(CT):
                    for k in range(UN):
                        u = UB * b + c * UN + k
                        pool.wait_ge(S["scanned"], u + 1)
                        if c == 0 and k % 2 == 0:
                            pool.wait_ge(c_in[k // 2], 16 * (b + 1))
                        w = work[:, (c * UN + k) % WR, :, :]
                        pool.tensor_tensor(w, w, c_bc[:, NU * k:NU * (k + 1), :], ALU.mult).then_inc(S["hc_done"], 1)
                        if k == 0:
                            if c > 0:
                                gate(b, par, c - 1)
                            elif not first:
                                gate(b - 1, 1 - par, CT - 1)
                        if k == 3 and not (last and c == CT - 1):
                            add_dt(CT * b + c + 1, (c + 1) % CT)
                        if not first and c < 2 and k in (5, 7):
                            residual(b - 1, 2 * c + (k == 7))

            l1_iterations(pool, l1)
            gate(B - 1, (B - 1) % 2, CT - 1)
            for t in range(TT):
                residual(B - 1, t)


IN = ("x", "mask", "cond", "cols", "wk", "wq", "wv", "wo", "bq", "bv", "b_out", "w_emb", "w_ada", "gate_b",
      "w_in", "w_out2", "w_xp", "w_dt")


def kernel(**inputs):
    import numpy as np
    import concourse.bacc as bacc
    from concourse.bass_utils import run_bass_kernel_spmd

    a = {k: np.asarray(v) for k, v in inputs.items()}
    L0, L1 = "L0_cond_", "L1_cond_"

    def col(v):
        return v.reshape(-1, 128).T

    def col2(w):
        return w.reshape(-1, 128, w.shape[1]).transpose(1, 0, 2).reshape(128, -1)

    B, T, D = a["x"].shape
    cols = np.concatenate([
        col(a[L0 + "ln_w"]), col(a[L0 + "ln_b"]), col(a[L0 + "bk"]), col(a[L0 + "b_emb"]), col(a[L0 + "ln2_w"]),
        col(a[L0 + "ln2_b"]), col(a[L1 + "ln_g"]), col(a[L1 + "ln_b"]), col(a[L1 + "ada_b"]), col2(a[L1 + "conv_w"]),
        col(a[L1 + "conv_b"]), col(a[L1 + "dt_proj_b"]), col2(a[L1 + "A_log"]), col(a[L1 + "D_param"]),
        col(a["mask_BxSx1_fk1"].reshape(-1))], axis=1)
    arrays = {
        "x": a["x"], "mask": a["mask_BxSx1_fk1"].reshape(B, T),
        "cond": a["cond_2048"].reshape(B, -1, 128).transpose(2, 1, 0), "cols": cols,
        "wk": a[L0 + "Wk"], "wq": a[L0 + "Wq"], "wv": a[L0 + "Wv"], "wo": a[L0 + "W_out"],
        "bq": a[L0 + "bq"], "bv": a[L0 + "bv"], "b_out": a[L0 + "b_out"], "w_emb": a[L0 + "W_emb"],
        "w_ada": a[L1 + "ada_w"].T, "gate_b": a[L1 + "ada_b"][2 * D:],
        "w_in": a[L1 + "in_proj_w"].T, "w_out2": a[L1 + "out_proj_w"].T, "w_xp": a[L1 + "x_proj_w"].T,
        "w_dt": a[L1 + "dt_proj_w"].T}
    nc = bacc.Bacc("TRN2", target_bir_lowering=False, num_devices=1)
    d = {}
    for name in IN:
        arrays[name] = np.ascontiguousarray(arrays[name])
        d[name] = nc.dram_tensor("in_" + name, arrays[name].shape, F32, kind="ExternalInput").ap()
    d["out"] = nc.dram_tensor("out", (B, T, D), F32, kind="ExternalOutput").ap()
    d["x1"] = nc.dram_tensor("x1_d", (B, T, D), F32, kind="Internal").ap()
    d["xh"] = nc.dram_tensor("xh_d", (B, D, T), F32, kind="Internal").ap()
    d["bc_d"] = nc.dram_tensor("bc_d", (32, T), F32, kind="Internal").ap()
    d["gate_d"] = nc.dram_tensor("gate_d", (B, D), F32, kind="Internal").ap()
    build(nc, d)
    r = run_bass_kernel_spmd(nc, [{"in_" + n: arrays[n] for n in IN}], core_ids=[0])
    return r.results[0]["out"]
```

```python
from contextlib import ExitStack

import concourse.bass as bass
from concourse import mybir

F32 = mybir.dt.float32
ALU = mybir.AluOpType
ACT = mybir.ActivationFunctionType
AX = mybir.AxisListType

P = 128
EPS = 1e-5
MASK_BIAS = 1e6


def build(nc, d):
    B, T, D = d["x"].shape
    TT, DT = T // P, D // P
    H = 8
    DH = D // H
    PAIRS = H // 2
    KC = d["cond"].shape[1]
    DI = d["w_out2"].shape[0]
    CT = DI // P
    N = 16
    R = 64
    XP = R + 2 * N
    NU = 2
    UN = N // NU
    NG = 4
    GN = N // NG
    WR = 4
    UB = CT * UN
    assert (TT, DT, CT, XP) == (4, 4, 8, 96)

    col, at = {}, 0
    for name, n in (("ln_w", DT), ("ln_b", DT), ("bk", DT), ("b_emb", 2 * DT), ("ln2_w", DT), ("ln2_b", DT),
                    ("g1", DT), ("b1", DT), ("b_ada", 3 * DT), ("conv_w", 4 * CT), ("conv_b", CT),
                    ("dt_b", CT), ("a_log", N * CT), ("d_par", CT), ("mask", B * TT)):
        col[name] = at
        at += n
    NCOL = at
    assert NCOL == d["cols"].shape[1]

    ctx = ExitStack()
    with ctx:
        def sb(name, n):
            return ctx.enter_context(nc.sbuf_tensor(name, [P, n], F32))

        def sem(name):
            return ctx.enter_context(nc.semaphore(name))

        cols = sb("cols", NCOL)
        ident = sb("ident", P)
        cond = sb("cond_sb", KC * B)
        embv = sb("embv", 2 * DT * B)
        adav = sb("adav", 2 * DT * B)
        scale0 = sb("scale0", B * DT)
        shift0 = sb("shift0", B * DT)
        scale1 = sb("scale1", B * DT)
        shift1 = sb("shift1", B * DT)
        cur = sb("cur", 5 * DT)
        neg_a = sb("neg_a", N * CT)
        stats = sb("stats", TT * 6)
        mv = sb("mv", TT * 2)
        rstd = sb("rstd", TT)
        nmr = sb("nmr", TT)
        minus_half = sb("minus_half", TT)
        spare = sb("spare", 1)
        eps_col = sb("eps_col", TT)
        zero_col = sb("zero_col", TT)
        var_eps = sb("var_eps", TT)
        stats3 = sb("stats3", TT * 6)
        mv3 = sb("mv3", TT * 2)
        rstd3 = sb("rstd3", TT)
        nmr3 = sb("nmr3", TT)
        stats2 = sb("stats2", TT * 6)
        mv2 = sb("mv2", TT * 2)
        rstd2 = sb("rstd2", TT)
        nmr2 = sb("nmr2", TT)

        w2 = sb("w2", DT * 2 * DI + CT * D + CT * XP + DI)
        w_ada = w2[:, 0:KC * 3 * D].rearrange("p (k n) -> p k n", k=KC)
        o = 0
        w_in = w2[:, o:o + DT * 2 * DI].rearrange("p (k n) -> p k n", k=DT)
        o += DT * 2 * DI
        w_out2 = w2[:, o:o + CT * D].rearrange("p (k n) -> p k n", k=CT)
        o += CT * D
        w_xp = w2[:, o:o + CT * XP].rearrange("p (k n) -> p k n", k=CT)
        o += CT * XP
        w_dt = w2[0:R, o:o + DI]

        TD = TT * D
        ARENA = 37888
        arena = sb("arena", ARENA)

        def views(*sizes):
            out, o = [], 0
            for n in sizes:
                out.append(arena[:, o:o + n])
                o += n
            assert o <= ARENA, o
            return out

        tiled = lambda a, k: a.rearrange("p (k n) -> p k n", k=k)
        (a_wk, a_wq, a_wv, a_wo, a_xr, a_sT, a_xh, a_xhT, a_xn, a_xnT, a_ekT, a_ek, a_q, a_eqT, a_v, a_y,
         a_att, bq_bc, bv_bc, bo_bc, maskrow, gate_sb, gate_b, a_sm) = views(
            *[DT * D] * 4, *[TD] * 12, PAIRS * P, D, D, D, T, D, D, 128)
        assert KC * 2 * D == 4 * TD
        a_wemb = arena[:, 4 * DT * D:4 * DT * D + 4 * TD]
        wk, wq, wv, wo = (tiled(a, DT) for a in (a_wk, a_wq, a_wv, a_wo))
        w_emb = tiled(a_wemb, KC)
        xn, xr, xh, ek, q_sb, v_sb, y_sb = (tiled(a, TT) for a in (a_xn, a_xr, a_xh, a_ek, a_q, a_v, a_y))
        xnT, ekT, eqT, sT, xhT = (tiled(a, DT) for a in (a_xnT, a_ekT, a_eqT, a_sT, a_xhT))
        att = tiled(a_att, PAIRS)
        nkmax, ksum, rksum = a_sm[:, 0:4], a_sm[:, 4:8], a_sm[:, 8:12]
        nqmax = a_sm[:, 16:48].rearrange("p (t h) -> p t h", t=TT)
        qsum = a_sm[:, 48:80].rearrange("p (t h) -> p t h", t=TT)
        rqsum = a_sm[:, 80:112].rearrange("p (t h) -> p t h", t=TT)

        (a_uy0, a_xmT0, a_bb, a_cb, a_uy1, xd, sp, a_dt, a_sz, a_work, a_xmT1, a_res, gate_bc, o_tmp) = views(
            CT * T, TD, N * T, N * T, CT * T, T, T, 2 * T, 2 * T, WR * NU * T, TD, 2 * D, D, D)
        assert CT * T + TD == 3 * DT * D
        b_bc, c_bc = tiled(a_bb, N), tiled(a_cb, N)
        uy = [tiled(a, CT) for a in (a_uy0, a_uy1)]
        work = a_work.rearrange("p (w n t) -> p w n t", w=WR, n=NU)
        xmT = [tiled(a, DT) for a in (a_xmT0, a_xmT1)]
        res, sz, dt = (tiled(a, 2) for a in (a_res, a_sz, a_dt))

        bankA = ctx.enter_context(nc.psum_tensor("bankA", [P, 4, 512], F32))
        bankB = ctx.enter_context(nc.psum_tensor("bankB", [P, 4, 512], F32))
        dA = bankA[:, :, :].rearrange("p (s n) t -> p s n t", s=2)
        dtu, ybank = bankB[:, 0, :], bankB[:, 1, :]
        gbank = [bankB[:, 2, :], bankB[:, 3, :]]

        S = {n: sem(n) for n in (
            "cols_in", "cond_in", "bc_in", "gate_b_in", "wk_in", "wq_in", "wv_in", "wo_in", "wemb_in", "wada_in", "w2_in",
            "ident_made", "sync_passed", "pre_step", "cond_act", "emb_mm", "ada_mm", "emb_col", "ada_col", "gate_row", "gate_stored", "nega",
            "x_in", "xr_in", "mask_in", "ln_step", "xn_done", "xnT_mm", "xnT_sb", "kT_mm", "kb_done", "kmax_done", "k_exp",
            "yT_mm", "sT_done", "cur0_set", "curm_set", "q_mm", "q_biased", "q_max", "q_shift", "q_exp", "q_sum", "q_rec", "wo_mm", "xr_biased",
            "x1_done", "x1_stored", "ln3_step", "ln_norm", "ln2_norm", "ln3_norm", "half_made", "xh_done", "xhT_mm", "xhT_sb", "xh_stored", "v_mm", "v_done", "mbv_done", "maskb_done", "ekt_mm", "ek_sb", "k_rec", "eqT_mm", "eqT_sb",
            "att_mm", "att_sb", "y_mm", "y_sb", "ln2_step", "yn_done",
            "dA_zeroed", "a_ready", "bx_done", "scanned", "hc_step", "hc_done", "reduced", "y_raw", "y_done", "dtu_done", "sp_step", "dt_done",
            "sz_done", "filled0", "filled1", "freed0", "freed1", "conv_a", "conv_tap", "u_done", "xm_in", "gbc_in",
            "xmT_done", "cur1_set", "xd_done", "bcd_stored", "o_scaled", "res_added")}
        res_in, out_stored = [sem("res_in0"), sem("res_in1")], [sem("out_stored0"), sem("out_stored1")]
        b_in, c_in = [sem(f"b_in{g}") for g in range(NG)], [sem(f"c_in{g}") for g in range(NG)]
        filled, freed = [S["filled0"], S["filled1"]], [S["freed0"], S["freed1"]]

        STEPS = [["D1", "Z1", "O0"], ["D2", "O1", "O2"], ["D3", "Z2", "O3", "I0"], ["D4", "I1", "Z3", "I2", "I3"],
                 ["D5", "I4", "Z4", "I5", "I6"], ["D6", "I7", "Z5"], ["D7", "Z6", "P"], ["D8", "Z7", "Z8"]]
        assert STEPS[-1][-1] == f"Z{CT}"
        ADDED = [(c, 1) for c in range(CT)]
        PRODUCTS = {"D": 1, "Z": DT, "O": CT, "I": DT, "P": CT}

        def has(name, first, last):
            return not (first and name[0] == "O") and not (last and (name[0] in "IP" or name[1:] == str(CT)))

        def batch_jobs(first, last):
            return [n for step in STEPS for n in step if has(n, first, last)]

        def spread(c, first, last):
            seq = []
            for n in STEPS[c]:
                if has(n, first, last):
                    seq += [(n, k) for k in range(PRODUCTS[n[0]])]
            share = max(len(seq), 3 * UN // 2)
            return [[x for n, x in enumerate(seq) if n * UN // share == k] for k in range(UN)]

        def read_at(late, kinds, first, last):
            out = [[] for _ in range(UB)]
            for c in range(CT):
                for e, part in enumerate(spread(c, first, last)):
                    for name, k in part:
                        if k == PRODUCTS[name[0]] - 1 and name[0] in kinds and name != f"Z{CT}":
                            out[min(c * UN + e + late, UB - 1)].append(name)
            return out

        DVE_AHEAD, ACT_AHEAD, POOL_AHEAD = 3, 4, 3

        JOBS_A_BATCH = len(batch_jobs(False, False))
        number, n = {}, 0
        pre = [f"I{j}" for j in range(CT)] + ["P", "D0", "Z0"]
        for copy, jobs in (("pre", pre), ("first", batch_jobs(True, False)), ("odd", batch_jobs(False, False)),
                           ("even", batch_jobs(False, False))):
            for j in jobs:
                number[copy, j] = n
                n += 1
        n += (B // 2 - 2) * 2 * JOBS_A_BATCH
        for copy, jobs in (("last", batch_jobs(False, True)), ("post", ["O0", "O1", "O2", "O3"])):
            for j in jobs:
                number[copy, j] = n
                n += 1

        def job(copy, it, name):
            n = number[copy, name] if (copy, name) in number else number[copy, "D1"] - 1
            k = n // 2
            return n % 2, (it * JOBS_A_BATCH + k if copy in ("odd", "even") else k)

        COPIES_LOOP = [("odd", 1), ("even", 2)]

        def l0_iterations(eng, body):
            body(0, False, True, True)
            body(1, True, True, True)
            with eng.Fori(2, B - 1) as i:
                body(i, True, True, True)
            body(B - 1, True, True, False)
            body(B, True, False, False)

        def l1_iterations(eng, body):
            body("first", 0, 0, 0, True, False)
            with eng.Fori(0, B // 2 - 1) as it:
                for copy, off in COPIES_LOOP:
                    body(copy, it, it * 2 + off, off % 2, False, False)
            body("last", 0, B - 1, (B - 1) % 2, False, True)

        def started(b):
            return not (isinstance(b, int) and b == 0)

        BY_LAST_USE = (1, 2, 3, 0)

        def second(b):
            return isinstance(b, int) and b == 1

        block = ctx.enter_context(nc.Block())

        @block.sync
        def _(sp_):
            sp_.dma_start(cols[:, :], d["cols"]).then_inc(S["cols_in"], 16)
            sp_.dma_start(xn, d["x"][0].rearrange("(t p) n -> p t n", p=P)).then_inc(S["x_in"], 16)
            for w, name, s in ((wk, "wk", "wk_in"), (wq, "wq", "wq_in"), (wv, "wv", "wv_in")):
                sp_.dma_start(w, d[name].rearrange("(k p) n -> p k n", p=P)).then_inc(S[s], 16)
            for t, name in ((bq_bc, "bq"), (bv_bc, "bv"), (bo_bc, "b_out")):
                sp_.dma_start(t, d[name].rearrange("(a n) -> a n", a=1).to_broadcast([P, D])).then_inc(S["bc_in"], 16)
            sp_.dma_start(cond[:, :], d["cond"].rearrange("p k b -> p (k b)")).then_inc(S["cond_in"], 16)

            def later_weights():
                sp_.dma_start(w_emb, d["w_emb"].rearrange("(k p) n -> p k n", p=P)).then_inc(S["wemb_in"], 16)
                sp_.dma_start(wo, d["wo"].rearrange("(k p) n -> p k n", p=P)).then_inc(S["wo_in"], 16)
                sp_.dma_start(gate_b[0:B, :], d["gate_b"].rearrange("(a n) -> a n", a=1).to_broadcast([B, D])).then_inc(S["gate_b_in"], 16)
                sp_.dma_start(w_ada, d["w_ada"].rearrange("(k p) n -> p k n", p=P)).then_inc(S["wada_in"], 16)

            def second_weights():
                sp_.wait_ge(S["gate_row"], 1)
                sp_.dma_start(d["gate_d"], gate_sb[0:B, :]).then_inc(S["gate_stored"], 16)
                sp_.dma_start(w_in, d["w_in"].rearrange("(k p) n -> p k n", p=P)).then_inc(S["w2_in"], 16)
                sp_.dma_start(w_out2, d["w_out2"].rearrange("(k p) n -> p k n", p=P)).then_inc(S["w2_in"], 16)
                sp_.dma_start(w_xp, d["w_xp"].rearrange("(k p) n -> p k n", p=P)).then_inc(S["w2_in"], 16)
                sp_.dma_start(w_dt, d["w_dt"]).then_inc(S["w2_in"], 16)

            def l0(i, prev, cur_, nxt):
                if cur_:
                    if started(i):
                        sp_.wait_ge(S["kb_done"], DT * i)
                        sp_.sem_inc(S["sync_passed"], 1)
                    sp_.dma_start(maskrow, d["mask"][bass.ds(i, 1), :].to_broadcast([P, T])).then_inc(S["mask_in"], 16)
                if nxt:
                    sp_.wait_ge(S["xnT_mm"], DT * (i + 1))
                    sp_.sem_inc(S["sync_passed"], 1)
                    sp_.dma_start(xn, d["x"][bass.ds(i + 1, 1), :, :].rearrange("a (t p) n -> p (a t) n", p=P)).then_inc(S["x_in"], 16)
                if not started(i):
                    later_weights()
                if prev:
                    if second(i):
                        sp_.wait_ge(S["emb_mm"], 1)
                    else:
                        sp_.wait_ge(S["x1_stored"], 16 * (i - 1))
                        sp_.sem_inc(S["sync_passed"], 1)
                        sp_.wait_ge(S["xh_done"], TT * (i - 1))
                        sp_.sem_inc(S["sync_passed"], 1)
                    sp_.dma_start(xr, d["x"][bass.ds(i - 1, 1), :, :].rearrange("a (t p) n -> p (a t) n", p=P)).then_inc(S["xr_in"], 16)
                if second(i):
                    second_weights()
                if cur_ and not nxt:
                    sp_.wait_ge(S["v_mm"], TT * B)
                    sp_.wait_ge(S["xh_stored"], 16)
                    load_xm(0, 0)
                if prev:
                    sp_.wait_ge(S["x1_done"], TT * i)
                    sp_.sem_inc(S["sync_passed"], 1)
                    sp_.dma_start(d["x1"][bass.ds(i - 1, 1), :, :].rearrange("a (t p) n -> p (a t) n", p=P), xr).then_inc(S["x1_stored"], 16)
                    sp_.wait_ge(S["xhT_sb"], DT * i)
                    sp_.sem_inc(S["sync_passed"], 1)
                    sp_.dma_start(d["xh"][bass.ds(i - 1, 1), :, :].rearrange("a (m p) t -> p (a m) t", p=P), xhT).then_inc(S["xh_stored"], 16)

            def load_xm(b, par):
                sp_.dma_start(xmT[par], d["xh"][bass.ds(b, 1), :, :].rearrange("a (m p) t -> p (a m) t", p=P)).then_inc(S["xm_in"], 16)

            def load_bc(b):
                sp_.wait_ge(S["xd_done"], b + 1)
                sp_.sem_inc(S["sync_passed"], 1)
                sp_.dma_start(d["bc_d"], xd[R:XP, :]).then_inc(S["bcd_stored"], 16)
                sp_.wait_ge(S["bcd_stored"], 16 * (b + 1))
                sp_.sem_inc(S["sync_passed"], 1)
                for g in range(NG):
                    rows = d["bc_d"].rearrange("n t -> (n t)").rearrange("(a m) -> a m", a=1)
                    if started(b):
                        sp_.wait_ge(S["bx_done"], UB * b - UN + 2 * (g + 1))
                        sp_.sem_inc(S["sync_passed"], 1)
                    sp_.dma_start(a_bb[:, g * GN * T:(g + 1) * GN * T], rows[:, g * GN * T:(g + 1) * GN * T].to_broadcast([P, GN * T])).then_inc(b_in[g], 16)
                    if started(b):
                        sp_.wait_ge(S["hc_done"], UB * b - UN + 2 * (g + 1))
                        sp_.sem_inc(S["sync_passed"], 1)
                    sp_.dma_start(a_cb[:, g * GN * T:(g + 1) * GN * T], rows[:, (N + g * GN) * T:(N + (g + 1) * GN) * T].to_broadcast([P, GN * T])).then_inc(c_in[g], 16)

            def outputs(b):
                rows = lambda name, t: d[name][bass.ds(b, 1), t * P:(t + 1) * P, :].rearrange("a p n -> p (a n)")
                if started(b):
                    sp_.wait_ge(S["o_scaled"], TT * b)
                    sp_.sem_inc(S["sync_passed"], 1)
                sp_.dma_start(gate_bc, d["gate_d"][bass.ds(b, 1), :].to_broadcast([P, D])).then_inc(S["gbc_in"], 16)
                for t in range(TT + 1):
                    if t < TT:
                        if t >= 2 or started(b):
                            sp_.wait_ge(out_stored[t % 2], 16 * (2 * b + t // 2))
                            sp_.sem_inc(S["sync_passed"], 1)
                        sp_.dma_start(res[:, t % 2, :], rows("x1", t)).then_inc(res_in[t % 2], 16)
                    if t >= 1:
                        sp_.wait_ge(S["res_added"], TT * b + t)
                        sp_.sem_inc(S["sync_passed"], 1)
                        sp_.dma_start(rows("out", t - 1), res[:, (t - 1) % 2, :]).then_inc(out_stored[(t - 1) % 2], 16)

            l0_iterations(sp_, l0)
            sp_.wait_ge(S["x1_stored"], 16 * B)
            sp_.wait_ge(S["xh_stored"], 16 * B)
            sp_.wait_ge(S["gate_stored"], 16)
            load_bc(0)

            def l1(copy, it, b, par, first, last):
                if not last:
                    if not first:
                        sp_.wait_ge(S["reduced"], UB * b)
                        sp_.sem_inc(S["sync_passed"], 1)
                    load_xm(b + 1, 1 - par)
                if not first:
                    outputs(b - 1)
                if not last:
                    load_bc(b + 1)

            l1_iterations(sp_, l1)
            outputs(B - 1)
            for o in out_stored:
                sp_.wait_ge(o, 16 * 2 * B)

        @block.tensor
        def _(pe):
            def transposes(out, blocks):
                for k, blk in enumerate(blocks):
                    mm = pe.transpose(out[:, k * P:(k + 1) * P], blk, ident[:, :])
                return mm

            def product(out, lhs, rhs, kt):
                for k in range(kt):
                    mm = pe.matmul(out, lhs(k), rhs(k), start=(k == 0), stop=(k == kt - 1))
                return mm

            def conditions():
                pe.wait_ge(S["cond_act"], 1)
                pe.wait_ge(S["wemb_in"], 16)
                pe.wait_ge(S["xnT_sb"], 2 * DT)
                cv = cond[:, :].rearrange("p (k b) -> p k b", k=KC)
                for m in range(2 * DT):
                    mm = product(bankA[:, 1, m * B:(m + 1) * B], lambda k: w_emb[:, k, m * P:(m + 1) * P], lambda k: cv[:, k, :], KC)
                mm.then_inc(S["emb_mm"], 1)
                pe.wait_ge(S["wada_in"], 16)
                for m in range(2 * DT):
                    product(bankA[:, 2, m * B:(m + 1) * B], lambda k: w_ada[:, k, m * P:(m + 1) * P], lambda k: cv[:, k, :], KC)
                product(bankA[0:B, 3, :], lambda k: cv[:, k, :], lambda k: w_ada[:, k, 2 * D:3 * D], KC).then_inc(S["ada_mm"], 1)

            def next_norm(i):
                pe.wait_ge(S["xh_done"], TT * i)
                for m in BY_LAST_USE:
                    if m == 0 and not (isinstance(i, int) and i == B):
                        pe.wait_ge(S["att_sb"], 2 * (i + 1))
                    transposes(bankA[:, m, :], [xh[:, t, m * P:(m + 1) * P] for t in range(TT)]).then_inc(S["xhT_mm"], 1)

            def transpose_x(i, n):
                m = BY_LAST_USE[n]
                if n == 0:
                    pe.wait_ge(S["xn_done"], TT * (i + 1))
                transposes(bankA[:, m, :], [xn[:, t, m * P:(m + 1) * P] for t in range(TT)]).then_inc(S["xnT_mm"], 1)

            def l0(i, prev, cur_, nxt):
                begun = started(i)
                if cur_:
                    pe.wait_ge(S["xnT_sb"], DT * (i + 1))
                    if not begun:
                        pe.wait_ge(S["wk_in"], 16)
                    for m in range(DT):
                        if begun:
                            pe.wait_ge(S["y_sb"], TT * (i - 1) + m + 1)
                        product(bankB[:, m, :], lambda k: wk[:, k, m * P:(m + 1) * P], lambda k: xnT[:, k, :], DT).then_inc(S["kT_mm"], 1)
                if prev:
                    if not cur_:
                        pe.wait_ge(S["w2_in"], 64)
                        pe.wait_ge(S["y_sb"], TT * i)
                        whole("pre", 0, 0, ["I0", "I1", "I2"])
                        pe.wait_ge(S["xhT_sb"], DT * (i - 1))
                    pe.wait_ge(S["yn_done"], TT * i)
                    for m in range(DT):
                        transposes(bankA[:, m, :], [y_sb[:, t, m * P:(m + 1) * P] for t in range(TT)]).then_inc(S["yT_mm"], 1)
                    if not cur_:
                        whole("pre", 0, 0, ["I3"])
                if cur_:
                    if not begun:
                        pe.wait_ge(S["wq_in"], 16)
                    for t in range(TT):
                        pe.wait_ge(S["kb_done"], DT * i + t + 1)
                        product(bankB[:, t, :], lambda k: xnT[:, k, t * P:(t + 1) * P], lambda k: wq[:, k, :], DT).then_inc(S["q_mm"], 1)
                if prev:
                    pe.wait_ge(S["sT_done"], DT * i)
                    if second(i):
                        pe.wait_ge(S["wo_in"], 16)
                    for t in range(TT):
                        product(bankA[:, t, :], lambda k: sT[:, k, t * P:(t + 1) * P], lambda k: wo[:, k, :], DT).then_inc(S["wo_mm"], 1)
                if not cur_:
                    whole("pre", 0, 0, ["I4", "I5", "I6", "I7"])
                    pe.wait_ge(S["x1_done"], TT * i)
                    next_norm(i)
                    return
                if not begun:
                    pe.wait_ge(S["wv_in"], 16)
                for t in range(TT):
                    pe.wait_ge(S["q_biased"], TT * i + t + 1)
                    product(bankB[:, t, :], lambda k: xnT[:, k, t * P:(t + 1) * P], lambda k: wv[:, k, :], DT).then_inc(S["v_mm"], 1)
                pe.wait_ge(S["k_exp"], DT * (i + 1))
                for t in range(TT):
                    if prev:
                        pe.wait_ge(S["x1_done"], TT * (i - 1) + t + 1)
                    transposes(bankA[:, t, :], [ekT[:, m, t * P:(t + 1) * P] for m in range(DT)]).then_inc(S["ekt_mm"], 1)
                pe.wait_ge(S["q_exp"], TT * (i + 1))
                for m in range(DT):
                    pe.wait_ge(S["v_done"], TT * i + m + 1)
                    transposes(bankB[:, m, :], [q_sb[:, t, m * P:(m + 1) * P] for t in range(TT)]).then_inc(S["eqT_mm"], 1)
                pe.wait_ge(S["ek_sb"], TT * (i + 1))
                for h in range(PAIRS):
                    mm = product(bankA[:, 0, h * P:(h + 1) * P], lambda t: ek[:, t, h * P:(h + 1) * P],
                                 lambda t: v_sb[:, t, h * P:(h + 1) * P], TT)
                mm.then_inc(S["att_mm"], 1)
                if prev:
                    next_norm(i)
                pe.wait_ge(S["att_sb"], 2 * (i + 1))
                pe.wait_ge(S["eqT_sb"], DT * (i + 1))
                for t in range(TT):
                    for h in range(PAIRS):
                        mm = pe.matmul(bankB[:, t, h * P:(h + 1) * P], eqT[:, h, t * P:(t + 1) * P], att[:, h, :], start=True, stop=True)
                    mm.then_inc(S["y_mm"], 1)
                    if nxt:
                        if prev:
                            pe.wait_ge(S["xhT_sb"], DT * (i - 1) + t + 1)
                        transpose_x(i + 1, t)
                if not begun:
                    conditions_after(pe)

            def conditions_after(pe):
                conditions()
                pe.wait_ge(S["emb_col"], 1)
                pe.wait_ge(S["ada_col"], 1)
                pe.wait_ge(S["gate_row"], 1)

            def run(copy, it, b, par, name, ks):
                bank, before = job(copy, it, name)
                out = gbank[bank]
                kind, j = name[0], int(name[1:] or 0)
                nb, npar = (0, 0) if copy == "pre" else (b + 1, 1 - par)
                if ks[0] == 0:
                    if number[copy, name] >= 2:
                        pe.wait_ge(freed[bank], before)
                    if kind == "I" and j == 0:
                        pe.wait_ge(S["xmT_done"], DT * (nb + 1))
                    elif kind == "P":
                        pe.wait_ge(S["u_done"], CT * (nb + 1))
                    elif kind == "D" and j in (0, CT):
                        pe.wait_ge(S["xd_done"], nb + 1)
                    elif kind == "O" and j == 0:
                        pe.wait_ge(S["y_done"], CT * (b + 1 if copy == "post" else b))
                for k in ks:
                    ends = dict(start=(k == 0), stop=(k == PRODUCTS[kind] - 1))
                    if kind == "I":
                        mm = pe.matmul(out, w_in[:, k, j * P:(j + 1) * P], xmT[npar][:, k, :], **ends)
                    elif kind == "P":
                        mm = pe.matmul(out[0:XP, :], w_xp[:, k, :], uy[npar][:, k, :], **ends)
                    elif kind == "D":
                        c = j % CT
                        mm = pe.matmul(out, w_dt[:, c * P:(c + 1) * P], xd[0:R, :], **ends)
                    elif kind == "Z":
                        c = j % CT
                        zp = npar if copy == "pre" or j == CT else par
                        mm = pe.matmul(out, w_in[:, k, DI + c * P:DI + (c + 1) * P], xmT[zp][:, k, :], **ends)
                    else:
                        opar = par if copy == "post" else 1 - par
                        mm = pe.matmul(out, uy[opar][:, k, j * P:(j + 1) * P], w_out2[:, k, :], **ends)
                if ks[-1] == PRODUCTS[kind] - 1:
                    mm.then_inc(filled[bank], 1)

            def whole(copy, b, par, names):
                for name in names:
                    run(copy, 0, b, par, name, range(PRODUCTS[name[0]]))

            def l1(copy, it, b, par, first, last):
                for c in range(CT):
                    parts = spread(c, first, last)
                    for k in range(UN):
                        u = UB * b + c * UN + k
                        pe.wait_ge(S["hc_done"], u + 1)
                        if k == 0 and not (first and c == 0):
                            pe.wait_ge(S["y_raw"], CT * b + c)
                        states = 1 if (c, k) in ADDED else NU
                        for n in range(states):
                            mm = pe.matmul(ybank, ident[:, :], work[:, (c * UN + k) % WR, n, :],
                                           start=(k == 0 and n == 0), stop=(k == UN - 1 and n == states - 1))
                        mm.then_inc(S["reduced"], 1)
                        for name in dict.fromkeys(n for n, _ in parts[k]):
                            run(copy, it, b, par, name, [q for n, q in parts[k] if n == name])

            pe.wait_ge(S["ident_made"], 2)
            for n in range(DT):
                transpose_x(0, n)
            l0_iterations(pe, l0)
            whole("pre", 0, 0, ["P", "D0", "Z0"])
            l1_iterations(pe, l1)
            whole("post", B - 1, (B - 1) % 2, [f"O{t}" for t in range(TT)])

        @block.scalar
        def _(act):
            act.wait_ge(S["cols_in"], 16)
            act.activation(neg_a[:, :], cols[:, col["a_log"]:col["a_log"] + N * CT], ACT.Exp).then_inc(S["nega"], 1)

            def normalise0(i):
                act.wait_ge(S["ln_norm"], 4 * (i + 1))
                for t in range(TT):
                    act.activation(xn[:, t, :], xn[:, t, :], ACT.Identity, scale=rstd[:, t:t + 1], bias=nmr[:, t:t + 1]).then_inc(S["xn_done"], 1)

            def x_out(i):
                if started(i):
                    act.wait_ge(S["v_mm"], TT * i)
                for n, m in enumerate(BY_LAST_USE):
                    act.wait_ge(S["xnT_mm"], DT * i + n + 1)
                    act.activation(xnT[:, m, :], bankA[:, m, :], ACT.Identity, scale=cols[:, col["ln_w"] + m:col["ln_w"] + m + 1],
                                   bias=cols[:, col["ln_b"] + m:col["ln_b"] + m + 1]).then_inc(S["xnT_sb"], 1)

            def xh_out(i):
                for n, m in enumerate(BY_LAST_USE):
                    act.wait_ge(S["xhT_mm"], DT * (i - 1) + n + 1)
                    if n == 0 and not second(i):
                        act.wait_ge(S["xh_stored"], 16 * (i - 1))
                    act.activation(xhT[:, m, :], bankA[:, m, :], ACT.Identity).then_inc(S["xhT_sb"], 1)

            def l0(i, prev, cur_, nxt):
                if cur_:
                    if not started(i):
                        act.wait_ge(S["cond_in"], 16)
                        act.activation(cond[:, :], cond[:, :], ACT.Silu).then_inc(S["cond_act"], 1)
                    for m in range(DT):
                        act.wait_ge(S["kmax_done"], DT * i + m + 1)
                        act.activation(ekT[:, m, :], ekT[:, m, :], ACT.Exp, bias=nkmax[:, m:m + 1], accum_out=ksum[:, m:m + 1]).then_inc(S["k_exp"], 1)
                if prev and not cur_:
                    conv_starts(range(3))
                if prev:
                    act.wait_ge(S["cur0_set"], 2 * i)
                    for m in range(DT):
                        act.wait_ge(S["yT_mm"], DT * (i - 1) + m + 1)
                        if m == 0 and not second(i):
                            act.wait_ge(S["wo_mm"], TT * (i - 1))
                        act.activation(sT[:, m, :], bankA[:, m, :], ACT.Silu, scale=cur[:, m:m + 1], bias=cur[:, DT + m:DT + m + 1]).then_inc(S["sT_done"], 1)
                if prev and not cur_:
                    for j in range(3):
                        conv_silu(0, 0, j)
                    conv_starts(range(3, CT))
                if cur_:
                    for t in range(TT):
                        act.wait_ge(S["q_shift"], TT * i + t + 1)
                        act.activation(q_sb[:, t, :], q_sb[:, t, :], ACT.Exp).then_inc(S["q_exp"], 1)
                if nxt:
                    normalise0(i + 1)
                if prev:
                    act.wait_ge(S["ln3_norm"], 4 * i)
                    for t in range(TT):
                        if not second(i):
                            act.wait_ge(S["xhT_mm"], DT * (i - 1))
                        act.activation(xh[:, t, :], xr[:, t, :], ACT.Identity, scale=rstd3[:, t:t + 1], bias=nmr3[:, t:t + 1]).then_inc(S["xh_done"], 1)
                if cur_:
                    for m in range(DT):
                        act.wait_ge(S["eqT_mm"], DT * i + m + 1)
                        act.activation(eqT[:, m, :], bankB[:, m, :], ACT.Identity).then_inc(S["eqT_sb"], 1)
                    if prev:
                        xh_out(i)
                    if nxt:
                        x_out(i + 1)
                    else:
                        condition(0, 0)
                    act.wait_ge(S["ln2_norm"], 4 * (i + 1))
                    for t in range(TT):
                        act.activation(y_sb[:, t, :], y_sb[:, t, :], ACT.Identity, scale=rstd2[:, t:t + 1], bias=nmr2[:, t:t + 1]).then_inc(S["yn_done"], 1)
                else:
                    xh_out(i)

            def condition(b, par):
                act.wait_ge(S["cur1_set"], 2 * (b + 1))
                act.wait_ge(S["xm_in"], 16 * (b + 1))
                for m in range(DT):
                    act.activation(xmT[par][:, m, :], xmT[par][:, m, :], ACT.Identity, scale=cur[:, 3 * DT + m:3 * DT + m + 1],
                                   bias=cur[:, 4 * DT + m:4 * DT + m + 1]).then_inc(S["xmT_done"], 1)

            def conv_start(copy, it, name, b, npar):
                j = int(name[1])
                bank, before = job(copy, it, name)
                act.wait_ge(filled[bank], before + 1)
                act.activation(uy[npar][:, j, :], gbank[bank], ACT.Identity, scale=cols[:, col["conv_w"] + 4 * j + 3:col["conv_w"] + 4 * j + 4],
                               bias=cols[:, col["conv_b"] + j:col["conv_b"] + j + 1]).then_inc(S["conv_a"], 1)

            def conv_silu(b, npar, j):
                act.wait_ge(S["conv_tap"], 3 * (CT * b + j + 1))
                act.activation(uy[npar][:, j, :], uy[npar][:, j, :], ACT.Silu).then_inc(S["u_done"], 1)

            def evacuate_P(copy, it, b):
                bank, before = job(copy, it, "P")
                act.wait_ge(filled[bank], before + 1)
                if started(b):
                    act.wait_ge(S["bcd_stored"], 16 * b)
                act.activation(xd[0:XP, :], gbank[bank][0:XP, :], ACT.Identity).then_inc(S["xd_done"], 1)
                act.wait_ge(S["xd_done"], b + 1)
                act.sem_inc(freed[bank], 1)

            def softplus(copy, it, name, tile):
                bank, before = job(copy, it, name)
                c = int(name[1]) % CT
                bias = cols[:, col["dt_b"] + c:col["dt_b"] + c + 1]
                act.wait_ge(filled[bank], before + 1)
                if started(tile):
                    act.wait_ge(S["dt_done"], tile)
                    act.wait_ge(S["dtu_done"], tile)
                act.activation(dt[:, c % 2, :], gbank[bank], ACT.Relu, bias=bias)
                act.activation(sp, gbank[bank], ACT.Abs, bias=bias).then_inc(S["sp_step"], 1)
                act.wait_ge(S["sp_step"], 3 * tile + 1)
                act.sem_inc(freed[bank], 1)
                act.activation(sp, sp, ACT.Exp, scale=-1.0).then_inc(S["sp_step"], 1)

            def softplus_end(tile):
                act.wait_ge(S["sp_step"], 3 * tile + 2)
                act.activation(sp, sp, ACT.Ln, bias=1.0).then_inc(S["sp_step"], 1)

            def silu_z(copy, it, name, tile):
                bank, before = job(copy, it, name)
                act.wait_ge(filled[bank], before + 1)
                if not (isinstance(tile, int) and tile < 2):
                    act.wait_ge(S["y_done"], tile - 1)
                act.activation(sz[:, int(name[1]) % 2, :], gbank[bank], ACT.Silu).then_inc(S["sz_done"], 1)
                act.wait_ge(S["sz_done"], tile + 1)
                act.sem_inc(freed[bank], 1)

            def conv_starts(tiles):
                for j in tiles:
                    conv_start("pre", 0, f"I{j}", 0, 0)

            normalise0(0)
            x_out(0)
            l0_iterations(act, l0)
            for j in range(3, CT):
                conv_silu(0, 0, j)
            evacuate_P("pre", 0, 0)
            act.wait_ge(S["dA_zeroed"], 1)
            softplus("pre", 0, "D0", 0)
            softplus_end(0)

            def l1(copy, it, b, par, first, last):
                reads = read_at(ACT_AHEAD, "DIPZ", first, last)
                convs = read_at(DVE_AHEAD, "I", first, last)
                silus_to = 0
                for c in range(CT):
                    tile = CT * b + c
                    for k in range(UN):
                        u = UB * b + c * UN + k
                        if k == 0:
                            act.wait_ge(S["dt_done"], tile + 1)
                        if not (first and c == 0 and k < 2):
                            act.wait_ge(S["scanned"], u - 1)
                        for n in range(NU):
                            s = neg_a[:, c * N + NU * k + n:c * N + NU * k + n + 1]
                            e = act.activation(dA[:, k % 2, n, 1:T], dt[:, c % 2, 1:T], ACT.Exp, scale=s)
                        e.then_inc(S["a_ready"], 1)
                        for name in reads[c * UN + k]:
                            if name[0] == "D":
                                softplus(copy, it, name, CT * b + int(name[1]))
                                softplus_end(CT * b + int(name[1]))
                            elif name[0] == "I":
                                conv_start(copy, it, name, b + 1, 1 - par)
                            elif name[0] == "P":
                                evacuate_P(copy, it, b + 1)
                            else:
                                silu_z(copy, it, name, CT * b + int(name[1]))
                                unit = c * UN + k
                                for conv in convs[silus_to:unit]:
                                    for j in conv:
                                        conv_silu(b + 1, 1 - par, int(j[1]))
                                silus_to = unit
                        if c == 0 and k == 1:
                            silu_z(copy, it, "Z0", CT * b)
                        if k == 5 and not last and c == 1:
                            condition(b + 1, 1 - par)

            l1_iterations(act, l1)

        @block.vector
        def _(dve):
            def column(name, j):
                return cols[:, col[name] + j:col[name] + j + 1]

            def moments(src, st, m_v, s, before):
                for t in range(TT):
                    e = dve.bn_stats(st[:, 6 * t:6 * t + 6], src[:, t, :])
                e.then_inc(s, 1)
                dve.wait_ge(s, before + 1)
                dve.memset(spare[:, :], 0.0)
                for t in range(TT):
                    e = dve.bn_aggr(m_v[:, 2 * t:2 * t + 2], st[:, 6 * t:6 * t + 6])
                e.then_inc(s, 1)

            dve.memset(a_att, 0.0).then_inc(S["pre_step"], 1)
            dve.wait_ge(S["x_in"], 16)
            moments(xn, stats, mv, S["ln_step"], 0)
            dve.wait_ge(S["nega"], 1)
            dve.tensor_scalar(neg_a[:, :], neg_a[:, :], -1.0, None, ALU.mult).then_inc(S["nega"], 1)

            def columns():
                v = embv[:, :].rearrange("p (m b) -> p m b", m=2 * DT)
                a = adav[:, :].rearrange("p (m b) -> p m b", m=2 * DT)

                def vec(name, n=DT):
                    return cols[:, col[name]:col[name] + n].rearrange("p (m a) -> p m a", a=1).to_broadcast([P, n, B])

                dve.wait_ge(S["emb_mm"], 1)
                dve.tensor_tensor(v, bankA[:, 1, 0:2 * DT * B].rearrange("p (m b) -> p m b", b=B), vec("b_emb", 2 * DT), ALU.add).then_inc(S["emb_col"], 1)
                dve.wait_ge(S["ada_mm"], 1)
                dve.tensor_tensor(a, bankA[:, 2, 0:2 * DT * B].rearrange("p (m b) -> p m b", b=B), vec("b_ada", 2 * DT), ALU.add).then_inc(S["ada_col"], 1)
                dve.wait_ge(S["gate_b_in"], 16)
                dve.tensor_tensor(gate_sb[0:B, :], bankA[0:B, 3, :], gate_b[0:B, :], ALU.add).then_inc(S["gate_row"], 1)
                dve.wait_ge(S["emb_col"], 1)
                dve.wait_ge(S["ada_col"], 1)
                by_batch = lambda x: x[:, :].rearrange("p (b m) -> p m b", b=B)
                for n, (out_scale, out_shift, scale, shift, w, b) in enumerate((
                        (scale0, shift0, v[:, 0:DT, :], v[:, DT:, :], "ln2_w", "ln2_b"),
                        (scale1, shift1, a[:, DT:, :], a[:, 0:DT, :], "g1", "b1"))):
                    dve.tensor_scalar(scale, scale, 1.0, None, ALU.add).then_inc(S["pre_step"], 1)
                    dve.wait_ge(S["pre_step"], 4 * n + 2)
                    dve.tensor_tensor(by_batch(out_scale), scale, vec(w), ALU.mult).then_inc(S["pre_step"], 1)
                    dve.tensor_tensor(by_batch(out_shift), scale, vec(b), ALU.mult).then_inc(S["pre_step"], 1)
                    dve.wait_ge(S["pre_step"], 4 * n + 4)
                    dve.tensor_tensor(by_batch(out_shift), by_batch(out_shift), shift, ALU.add).then_inc(S["pre_step"], 1)
                dve.wait_ge(S["pre_step"], 9)

            def heads(x):
                return x.rearrange("p (h e) -> p h e", h=H)

            def spread(x, n):
                return x.rearrange("p (h a) -> p h a", a=1).to_broadcast([P, H, n])

            def l0(i, prev, cur_, nxt):
                begun = started(i)
                if prev:
                    if not second(i):
                        dve.wait_ge(S["sT_done"], DT * (i - 1))
                    dve.tensor_copy(cur[:, 0:DT], scale0[:, bass.ds((i - 1) * DT, DT)]).then_inc(S["cur0_set"], 1)
                    dve.tensor_copy(cur[:, DT:2 * DT], shift0[:, bass.ds((i - 1) * DT, DT)]).then_inc(S["cur0_set"], 1)
                if cur_:
                    if begun:
                        dve.wait_ge(S["mbv_done"], i)
                    else:
                        dve.wait_ge(S["cols_in"], 16)
                    dve.tensor_copy(cur[:, 2 * DT:3 * DT], cols[:, bass.ds(i * TT + col["mask"], TT)]).then_inc(S["curm_set"], 1)
                    dve.wait_ge(S["mask_in"], 16 * (i + 1))
                    dve.tensor_scalar(maskrow, maskrow, 1.0, MASK_BIAS, ALU.subtract, ALU.mult).then_inc(S["maskb_done"], 1)
                    for m in range(DT):
                        dve.wait_ge(S["kT_mm"], DT * i + m + 1)
                        if m == 0:
                            dve.wait_ge(S["maskb_done"], i + 1)
                            if begun:
                                dve.wait_ge(S["ekt_mm"], TT * i)
                        dve.scalar_tensor_tensor(ekT[:, m, :], bankB[:, m, :], column("bk", m), maskrow, ALU.add, ALU.add).then_inc(S["kb_done"], 1)
                        dve.wait_ge(S["kb_done"], DT * i + m + 1)
                        dve.tensor_reduce(nkmax[:, m:m + 1], ekT[:, m, :], AX.X, ALU.max, negate=True).then_inc(S["kmax_done"], 1)
                    for t in range(TT):
                        dve.wait_ge(S["q_mm"], TT * i + t + 1)
                        if t == 0:
                            dve.wait_ge(S["bc_in"], 48)
                            if begun:
                                dve.wait_ge(S["eqT_mm"], DT * i)
                        dve.tensor_tensor(q_sb[:, t, :], bankB[:, t, :], bq_bc, ALU.add).then_inc(S["q_biased"], 1)
                        dve.wait_ge(S["q_biased"], TT * i + t + 1)
                        dve.tensor_reduce(nqmax[:, t, :], heads(q_sb[:, t, :]), AX.X, ALU.max, negate=True).then_inc(S["q_max"], 1)
                if nxt:
                    dve.wait_ge(S["x_in"], 16 * (i + 2))
                    moments(xn, stats, mv, S["ln_step"], 2 * (i + 1))
                if prev and not cur_:
                    for j in range(CT // 2):
                        taps("pre", 0, f"I{j}", 0, 0)
                if prev:
                    dve.wait_ge(S["xr_biased"], i)
                    for t in range(TT):
                        dve.wait_ge(S["wo_mm"], TT * (i - 1) + t + 1)
                        dve.tensor_tensor(xr[:, t, :], bankA[:, t, :], xr[:, t, :], ALU.add).then_inc(S["x1_done"], 1)
                    dve.wait_ge(S["x1_done"], TT * i)
                    moments(xr, stats3, mv3, S["ln3_step"], 2 * (i - 1))
                if not cur_:
                    for j in range(CT // 2, CT):
                        taps("pre", 0, f"I{j}", 0, 0)
                    return
                dve.wait_ge(S["curm_set"], i + 1)
                for t in range(TT):
                    dve.wait_ge(S["v_mm"], TT * i + t + 1)
                    if t == 0:
                        dve.wait_ge(S["mbv_done"], i + 1)
                    dve.scalar_tensor_tensor(v_sb[:, t, :], bankB[:, t, :], cur[:, 2 * DT + t:2 * DT + t + 1], v_sb[:, t, :],
                                             ALU.mult, ALU.add).then_inc(S["v_done"], 1)
                dve.wait_ge(S["k_exp"], DT * (i + 1))
                dve.reciprocal(rksum, ksum).then_inc(S["k_rec"], 1)
                for t in range(TT):
                    dve.wait_ge(S["ekt_mm"], TT * i + t + 1)
                    dve.tensor_copy(ek[:, t, :], bankA[:, t, :]).then_inc(S["ek_sb"], 1)
                for t in range(TT):
                    dve.wait_ge(S["q_exp"], TT * i + t + 1)
                    dve.tensor_reduce(qsum[:, t, :], heads(q_sb[:, t, :]), AX.X, ALU.add).then_inc(S["q_sum"], 1)
                dve.wait_ge(S["q_sum"], TT * (i + 1))
                dve.reciprocal(a_sm[:, 80:112], a_sm[:, 48:80]).then_inc(S["q_rec"], 1)
                dve.wait_ge(S["att_mm"], i + 1)
                dve.wait_ge(S["k_rec"], i + 1)
                pa = bankA[:, 0, :].rearrange("p (h e) -> p h e", h=PAIRS)
                for s in range(2):
                    rows = slice(s * DH, (s + 1) * DH)
                    rk = rksum[rows, :].rearrange("p (h a) -> p h a", a=1).to_broadcast([DH, PAIRS, DH])
                    dve.tensor_tensor(att[rows, :, s * DH:(s + 1) * DH], pa[rows, :, s * DH:(s + 1) * DH], rk, ALU.mult).then_inc(S["att_sb"], 1)
                dve.wait_ge(S["q_rec"], i + 1)
                for t in range(TT):
                    dve.wait_ge(S["y_mm"], TT * i + t + 1)
                    dve.tensor_tensor(heads(y_sb[:, t, :]), heads(bankB[:, t, :]), spread(rqsum[:, t, :], DH), ALU.mult).then_inc(S["y_sb"], 1)
                dve.wait_ge(S["y_sb"], TT * (i + 1))
                moments(y_sb, stats2, mv2, S["ln2_step"], 2 * i)
                if not begun:
                    columns()
                    condition_columns(0)

            def condition_columns(b):
                if started(b):
                    dve.wait_ge(S["xmT_done"], DT * b)
                dve.tensor_copy(cur[:, 3 * DT:4 * DT], scale1[:, bass.ds(b * DT, DT)]).then_inc(S["cur1_set"], 1)
                dve.tensor_copy(cur[:, 4 * DT:5 * DT], shift1[:, bass.ds(b * DT, DT)]).then_inc(S["cur1_set"], 1)

            def taps(copy, it, name, b, npar):
                j = int(name[1])
                bank, before = job(copy, it, name)
                dve.wait_ge(S["conv_a"], CT * b + j + 1)
                u = uy[npar][:, j, :]
                for s in range(1, 4):
                    dve.scalar_tensor_tensor(u[:, s:T], gbank[bank][:, 0:T - s], column("conv_w", 4 * j + 3 - s), u[:, s:T],
                                             ALU.mult, ALU.add).then_inc(S["conv_tap"], 1)
                    dve.wait_ge(S["conv_tap"], 3 * (CT * b + j) + s)
                dve.sem_inc(freed[bank], 1)

            def make_dtu(b, par, c):
                tile = CT * b + c
                dve.wait_ge(S["dt_done"], tile + 1)
                if c == 0:
                    dve.wait_ge(S["u_done"], CT * (b + 1))
                if c or started(b):
                    dve.wait_ge(S["bx_done"], tile * UN)
                dve.tensor_tensor(dtu, dt[:, c % 2, :], uy[par][:, c, :], ALU.mult).then_inc(S["dtu_done"], 1)
                dve.wait_ge(S["dtu_done"], tile + 1)

            def times_b(b, c, k, started_):
                u = UB * b + c * UN + k
                if started_:
                    dve.wait_ge(S["reduced"], u - WR + 1)
                if c == 0 and k % 2 == 0:
                    dve.wait_ge(b_in[k // 2], 16 * (b + 1))
                two = dtu.rearrange("p (a t) -> p a t", a=1).to_broadcast([P, NU, T])
                dve.tensor_tensor(work[:, (c * UN + k) % WR, :, :], two, b_bc[:, NU * k:NU * (k + 1), :], ALU.mult).then_inc(S["bx_done"], 1)

            def gate_y(b, par, c):
                dve.wait_ge(S["reduced"], UB * b + (c + 1) * UN)
                dve.scalar_tensor_tensor(uy[par][:, c, :], uy[par][:, c, :], column("d_par", c), ybank, ALU.mult, ALU.add).then_inc(S["y_raw"], 1)

            def output(copy, it, name, b):
                t = int(name[1])
                bank, before = job(copy, it, name)
                dve.wait_ge(filled[bank], before + 1)
                if t == 0:
                    dve.wait_ge(S["gbc_in"], 16 * (b + 1))
                n = TT * b + t
                if t or started(b):
                    dve.wait_ge(S["res_added"], n)
                dve.tensor_tensor(o_tmp, gbank[bank], gate_bc, ALU.mult).then_inc(S["o_scaled"], 1)
                dve.wait_ge(S["o_scaled"], n + 1)
                dve.sem_inc(freed[bank], 1)

            l0_iterations(dve, l0)
            dve.wait_ge(S["xhT_sb"], DT * B)
            dve.memset(dA[:, :, :, 0:1], 0.0).then_inc(S["dA_zeroed"], 1)
            make_dtu(0, 0, 0)
            times_b(0, 0, 0, False)

            def l1(copy, it, b, par, first, last):
                reads = read_at(DVE_AHEAD, "IO", first, last)
                for c in range(CT):
                    for k in range(UN):
                        if k == 2:
                            if c > 0:
                                gate_y(b, par, c - 1)
                            elif not first:
                                gate_y(b - 1, 1 - par, CT - 1)
                        if k < UN - 1:
                            times_b(b, c, k + 1, not (first and c == 0 and k + 1 < WR))
                        elif c < CT - 1:
                            make_dtu(b, par, c + 1)
                            times_b(b, c + 1, 0, True)
                        elif not last:
                            make_dtu(b + 1, 1 - par, 0)
                            times_b(b + 1, 0, 0, True)
                        u = UB * b + c * UN + k
                        w = work[:, (c * UN + k) % WR, :, :].rearrange("p n t -> p (n t)")
                        dve.wait_ge(S["bx_done"], u + 1)
                        dve.wait_ge(S["a_ready"], u + 1)
                        dve.tensor_tensor_scan(w, dA[:, k % 2, :, :].rearrange("p n t -> p (n t)"), w, 0.0, ALU.mult, ALU.add).then_inc(S["scanned"], 1)
                        if not last and c == 0 and k == 2:
                            condition_columns(b + 1)
                        for name in reads[c * UN + k]:
                            if name[0] == "I":
                                taps(copy, it, name, b + 1, 1 - par)
                            else:
                                output(copy, it, name, b - 1)

            l1_iterations(dve, l1)
            gate_y(B - 1, (B - 1) % 2, CT - 1)
            for t in range(TT):
                output("post", 0, f"O{t}", B - 1)

        @block.gpsimd
        def _(pool):
            pool.memset(ident[:, :], 0.0).then_inc(S["ident_made"], 1)
            pool.wait_ge(S["ident_made"], 1)
            pool.affine_select(out=ident[:, :], in_=ident[:, :], compare_op=ALU.not_equal, fill=1.0, base=0,
                               pattern=[[-1, P]], channel_multiplier=1).then_inc(S["ident_made"], 1)
            pool.memset(minus_half[:, :], -0.5).then_inc(S["half_made"], 1)
            pool.memset(eps_col[:, :], EPS).then_inc(S["half_made"], 1)
            pool.memset(zero_col[:, :], 0.0).then_inc(S["half_made"], 1)
            pool.wait_ge(S["half_made"], 3)

            def norm_factors(m_v, rs, nm, made, s, n):
                pairs = m_v[:, :].rearrange("p (t two) -> p t two", two=2)
                pool.wait_ge(made, 2 * (n + 1))
                pool.tensor_tensor(var_eps[:, :], pairs[:, :, 1], eps_col[:, :], ALU.add).then_inc(s, 1)
                pool.wait_ge(s, 4 * n + 1)
                pool.tensor_tensor(rs[:, :], var_eps[:, :], minus_half[:, :], ALU.pow).then_inc(s, 1)
                pool.wait_ge(s, 4 * n + 2)
                pool.tensor_tensor(nm[:, :], pairs[:, :, 0], rs[:, :], ALU.mult).then_inc(s, 1)
                pool.wait_ge(s, 4 * n + 3)
                pool.tensor_tensor(nm[:, :], zero_col[:, :], nm[:, :], ALU.subtract).then_inc(s, 1)

            norm_factors(mv, rstd, nmr, S["ln_step"], S["ln_norm"], 0)
            pool.wait_ge(S["bc_in"], 48)

            def l0(i, prev, cur_, nxt):
                if cur_:
                    pool.wait_ge(S["curm_set"], i + 1)
                    if started(i):
                        pool.wait_ge(S["att_mm"], i)
                    for t in range(TT):
                        e = pool.tensor_tensor(v_sb[:, t, :], bv_bc, cur[:, 2 * DT + t:2 * DT + t + 1].to_broadcast([P, D]), ALU.mult)
                    e.then_inc(S["mbv_done"], 1)
                if prev:
                    pool.wait_ge(S["xr_in"], 16 * i)
                    pool.tensor_tensor(xr, xr, bo_bc.rearrange("p (a n) -> p a n", a=1).to_broadcast([P, TT, D]), ALU.add).then_inc(S["xr_biased"], 1)
                if cur_:
                    for t in range(TT):
                        pool.wait_ge(S["q_max"], TT * i + t + 1)
                        q = q_sb[:, t, :].rearrange("p (h e) -> p h e", h=H)
                        m = nqmax[:, t, :].rearrange("p (h a) -> p h a", a=1).to_broadcast([P, H, DH])
                        pool.tensor_tensor(q, q, m, ALU.add).then_inc(S["q_shift"], 1)
                if nxt:
                    norm_factors(mv, rstd, nmr, S["ln_step"], S["ln_norm"], i + 1)
                if prev:
                    norm_factors(mv3, rstd3, nmr3, S["ln3_step"], S["ln3_norm"], i - 1)
                if cur_:
                    norm_factors(mv2, rstd2, nmr2, S["ln2_step"], S["ln2_norm"], i)

            l0_iterations(pool, l0)

            def add_dt(tile, c):
                pool.wait_ge(S["sp_step"], 3 * (tile + 1))
                pool.tensor_tensor(dt[:, c % 2, :], dt[:, c % 2, :], sp, ALU.add).then_inc(S["dt_done"], 1)

            def gate(b, par, c):
                tile = CT * b + c
                pool.wait_ge(S["y_raw"], tile + 1)
                pool.wait_ge(S["sz_done"], tile + 1)
                pool.tensor_tensor(uy[par][:, c, :], uy[par][:, c, :], sz[:, c % 2, :], ALU.mult).then_inc(S["y_done"], 1)

            def residual(b, t):
                pool.wait_ge(S["o_scaled"], TT * b + t + 1)
                pool.wait_ge(res_in[t % 2], 16 * (2 * b + t // 2 + 1))
                pool.tensor_tensor(res[:, t % 2, :], res[:, t % 2, :], o_tmp, ALU.add).then_inc(S["res_added"], 1)

            add_dt(0, 0)

            def l1(copy, it, b, par, first, last):
                dts = read_at(ACT_AHEAD + 1, "D", first, last)
                outs = read_at(POOL_AHEAD, "O", first, last)
                for c in range(CT):
                    for k in range(UN):
                        u = UB * b + c * UN + k
                        pool.wait_ge(S["scanned"], u + 1)
                        if c == 0 and k % 2 == 0:
                            pool.wait_ge(c_in[k // 2], 16 * (b + 1))
                        w = work[:, (c * UN + k) % WR, :, :]
                        e = pool.tensor_tensor(w, w, c_bc[:, NU * k:NU * (k + 1), :], ALU.mult)
                        if (c, k) in ADDED:
                            e.then_inc(S["hc_step"], 1)
                            pool.wait_ge(S["hc_step"], len(ADDED) * b + ADDED.index((c, k)) + 1)
                            e = pool.tensor_tensor(w[:, 0, :], w[:, 0, :], w[:, 1, :], ALU.add)
                        e.then_inc(S["hc_done"], 1)
                        if k == 3:
                            if c > 0:
                                gate(b, par, c - 1)
                            elif not first:
                                gate(b - 1, 1 - par, CT - 1)
                        for name in dts[c * UN + k]:
                            add_dt(CT * b + int(name[1]), int(name[1]) % CT)
                        for name in outs[c * UN + k]:
                            residual(b - 1, int(name[1]))

            l1_iterations(pool, l1)
            gate(B - 1, (B - 1) % 2, CT - 1)
            for t in range(TT):
                residual(B - 1, t)


IN = ("x", "mask", "cond", "cols", "wk", "wq", "wv", "wo", "bq", "bv", "b_out", "w_emb", "w_ada", "gate_b",
      "w_in", "w_out2", "w_xp", "w_dt")


def kernel(**inputs):
    import numpy as np
    import concourse.bacc as bacc
    from concourse.bass_utils import run_bass_kernel_spmd

    a = {k: np.asarray(v) for k, v in inputs.items()}
    L0, L1 = "L0_cond_", "L1_cond_"

    def col(v):
        return v.reshape(-1, 128).T

    def col2(w):
        return w.reshape(-1, 128, w.shape[1]).transpose(1, 0, 2).reshape(128, -1)

    B, T, D = a["x"].shape
    cols = np.concatenate([
        col(a[L0 + "ln_w"]), col(a[L0 + "ln_b"]), col(a[L0 + "bk"]), col(a[L0 + "b_emb"]), col(a[L0 + "ln2_w"]),
        col(a[L0 + "ln2_b"]), col(a[L1 + "ln_g"]), col(a[L1 + "ln_b"]), col(a[L1 + "ada_b"]), col2(a[L1 + "conv_w"]),
        col(a[L1 + "conv_b"]), col(a[L1 + "dt_proj_b"]), col2(a[L1 + "A_log"]), col(a[L1 + "D_param"]),
        col(a["mask_BxSx1_fk1"].reshape(-1))], axis=1)
    arrays = {
        "x": a["x"], "mask": a["mask_BxSx1_fk1"].reshape(B, T),
        "cond": a["cond_2048"].reshape(B, -1, 128).transpose(2, 1, 0), "cols": cols,
        "wk": a[L0 + "Wk"], "wq": a[L0 + "Wq"], "wv": a[L0 + "Wv"], "wo": a[L0 + "W_out"],
        "bq": a[L0 + "bq"], "bv": a[L0 + "bv"], "b_out": a[L0 + "b_out"], "w_emb": a[L0 + "W_emb"],
        "w_ada": a[L1 + "ada_w"].T, "gate_b": a[L1 + "ada_b"][2 * D:],
        "w_in": a[L1 + "in_proj_w"].T, "w_out2": a[L1 + "out_proj_w"].T, "w_xp": a[L1 + "x_proj_w"].T,
        "w_dt": a[L1 + "dt_proj_w"].T}
    nc = bacc.Bacc("TRN2", target_bir_lowering=False, num_devices=1)
    d = {}
    for name in IN:
        arrays[name] = np.ascontiguousarray(arrays[name])
        d[name] = nc.dram_tensor("in_" + name, arrays[name].shape, F32, kind="ExternalInput").ap()
    d["out"] = nc.dram_tensor("out", (B, T, D), F32, kind="ExternalOutput").ap()
    d["x1"] = nc.dram_tensor("x1_d", (B, T, D), F32, kind="Internal").ap()
    d["xh"] = nc.dram_tensor("xh_d", (B, D, T), F32, kind="Internal").ap()
    d["bc_d"] = nc.dram_tensor("bc_d", (32, T), F32, kind="Internal").ap()
    d["gate_d"] = nc.dram_tensor("gate_d", (B, D), F32, kind="Internal").ap()
    build(nc, d)
    r = run_bass_kernel_spmd(nc, [{"in_" + n: arrays[n] for n in IN}], core_ids=[0])
    return r.results[0]["out"]
```
